# Optimizing a Trainium2 kernel written in Bass

```python
import numpy as np
import jax
import jax.numpy as jnp

def _softmax(x, axis=-1):
    return jax.nn.softmax(x, axis=axis)

def _gelu(x):
    return jax.nn.gelu(x, approximate=True)

def _silu(x):
    return jax.nn.silu(x)

def _sigmoid(x):
    return jax.nn.sigmoid(x)

def _layernorm(x, axis=-1, eps=1e-05):
    m = jnp.mean(x, axis=axis, keepdims=True)
    v = jnp.var(x, axis=axis, keepdims=True)
    return (x - m) / jnp.sqrt(v + eps)

def _scatter_add(tgt, idx, src, axis=0):
    return tgt.at[idx].add(src)

def _segment_sum(src, seg, n):
    return jax.ops.segment_sum(src, seg, n)
kernel_name = 'mk_seq_preln_d2_jaxref_r8_324211'

def setup_inputs(seed: int=0):
    np.random.seed(seed)
    _w = jnp.asarray

    def _L0_attn_setup():
        import jax, jax.numpy as jnp
        import numpy as np
        BATCH, SEQ, HID, INTER, NSTATE, DTRANK, KCONV = (1, 128, 256, 512, 16, 128, 4)
        EPS = 1e-06

        def _rms(x):
            x32 = x.astype(jnp.float32)
            return (x32 * jax.lax.rsqrt(jnp.mean(x32 * x32, axis=-1, keepdims=True) + EPS)).astype(x.dtype)
        key = jax.random.key(seed)
        ks = jax.random.split(key, 8)
        x = jax.random.normal(ks[0], (BATCH, SEQ, HID), jnp.float32)
        in_proj_w = jax.random.normal(ks[1], (HID, 2 * INTER), jnp.float32) * 0.02
        conv_w = jax.random.normal(ks[2], (INTER, 1, KCONV), jnp.float32) * 0.2
        conv_b = jnp.zeros((INTER,), jnp.float32)
        x_proj_w = jax.random.normal(ks[3], (INTER, DTRANK + 2 * NSTATE), jnp.float32) * 0.02
        dt_proj_w = jax.random.normal(ks[4], (DTRANK, INTER), jnp.float32) * DTRANK ** (-0.5)
        dt_proj_b = jax.random.normal(ks[5], (INTER,), jnp.float32) * 0.1
        out_proj_w = jax.random.normal(ks[6], (INTER, HID), jnp.float32) * 0.02
        A_log = jnp.log(jnp.broadcast_to(jnp.arange(1, NSTATE + 1, dtype=jnp.float32), (INTER, NSTATE)))
        D_param = jnp.ones((INTER,), jnp.float32)
        return {'x': x, 'in_proj_w': in_proj_w, 'conv_w': conv_w, 'conv_b': conv_b, 'x_proj_w': x_proj_w, 'dt_proj_w': dt_proj_w, 'dt_proj_b': dt_proj_b, 'out_proj_w': out_proj_w, 'A_log': A_log, 'D_param': D_param}
    _L0_attn_in = _L0_attn_setup()

    def _L0_ffn_setup():
        import jax, jax.numpy as jnp
        import numpy as np
        B_, S, D = (2, 256, 256)
        F_ = 1024
        R = 16
        H = 16
        HD = D // H
        MOD_SCALE = 0.1
        EPS = 1e-06

        def _rmsnorm(x, w):
            v = jnp.mean(x * x, axis=-1, keepdims=True)
            return x * jax.lax.rsqrt(v + EPS) * w

        def _attention(x, Wq, Wk, Wv, Wo):
            b, s, d = x.shape
            q = (x @ Wq.T).reshape(b, s, H, HD)
            k = (x @ Wk.T).reshape(b, s, H, HD)
            v = (x @ Wv.T).reshape(b, s, H, HD)
            scores = jnp.einsum('bqhd,bkhd->bhqk', q, k) / np.sqrt(HD).astype(np.float32)
            causal = jnp.tril(jnp.ones((s, s), bool))
            scores = jnp.where(causal, scores, jnp.finfo(scores.dtype).min)
            probs = jax.nn.softmax(scores, axis=-1)
            out = jnp.einsum('bhqk,bkhd->bqhd', probs, v).reshape(b, s, d)
            return out @ Wo.T
        key = jax.random.key(seed)
        ks = jax.random.split(key, 12)
        sd = 0.02
        return {'hidden_states': jax.random.normal(ks[0], (B_, S, D), jnp.float32), 'ln1_w': jnp.ones((D,), jnp.float32), 'ln2_w': jnp.ones((D,), jnp.float32), 'Wq': jax.random.normal(ks[1], (D, D), jnp.float32) * sd, 'Wk': jax.random.normal(ks[2], (D, D), jnp.float32) * sd, 'Wv': jax.random.normal(ks[3], (D, D), jnp.float32) * sd, 'Wo': jax.random.normal(ks[4], (D, D), jnp.float32) * sd, 'A': jax.random.normal(ks[5], (D, R), jnp.float32) * (0.01 / np.sqrt(D)), 'B': jax.random.normal(ks[6], (R, F_), jnp.float32) * (0.01 / np.sqrt(R)), 'W_in_base': jax.random.normal(ks[7], (F_, D), jnp.float32) * sd, 'W_up_base': jax.random.normal(ks[8], (F_, D), jnp.float32) * sd, 'W_down': jax.random.normal(ks[9], (D, F_), jnp.float32) * sd}
    _L0_ffn_in = _L0_ffn_setup()

    def _L1_attn_setup():
        import jax, jax.numpy as jnp
        import numpy as np
        NUM_HEADS = 4
        HEAD_K = 32
        HEAD_V = 64
        CHUNK = 64
        GATE_NORMALIZER = 16.0
        EPS = 1e-05

        def _gla_chunk(q, k, v, gk):
            B, H, S, Dk = q.shape
            Dv = v.shape[-1]
            N = S // CHUNK
            scale = Dk ** (-0.5)

            def to_chunks(x):
                return x.reshape(B, H, N, CHUNK, x.shape[-1]).transpose(2, 0, 1, 3, 4)
            qc, kc, vc, gkc = map(to_chunks, (q, k, v, gk))
            gc = jnp.cumsum(gkc, axis=-2)
            tri = jnp.tril(jnp.ones((CHUNK, CHUNK), dtype=q.dtype))

            def step(Sstate, xs):
                qi, ki, vi, gi = xs
                q_g = qi * jnp.exp(gi) * scale
                k_g = ki * jnp.exp(-gi)
                A = jnp.einsum('bhid,bhjd->bhij', q_g, k_g) * tri
                o_intra = jnp.einsum('bhij,bhjе->bhiе'.replace('е', 'e'), A, vi)
                o_inter = jnp.einsum('bhcd,bhde->bhce', q_g, Sstate)
                g_last = gi[:, :, -1, :]
                k_dec = ki * jnp.exp(g_last[:, :, None, :] - gi)
                S_new = Sstate * jnp.exp(g_last)[..., None] + jnp.einsum('bhcd,bhce->bhde', k_dec, vi)
                return (S_new, o_intra + o_inter)
            S0 = jnp.zeros((B, H, Dk, Dv), dtype=q.dtype)
            _, o = jax.lax.scan(step, S0, (qc, kc, vc, gc))
            return o.transpose(1, 2, 0, 3, 4).reshape(B, H, S, Dv)
        key = jax.random.key(seed)
        ks = jax.random.split(key, 10)
        B, S, Hd = (2, 256, 256)
        key_dim = NUM_HEADS * HEAD_K
        value_dim = NUM_HEADS * HEAD_V
        lr = 16
        w = lambda k, shp: jax.random.normal(k, shp, dtype=jnp.float32) * 0.02
        return {'hidden_states': jax.random.normal(ks[0], (B, S, Hd), dtype=jnp.float32), 'Wq': w(ks[1], (Hd, key_dim)), 'Wk': w(ks[2], (Hd, key_dim)), 'Wv': w(ks[3], (Hd, value_dim)), 'Wgk1': w(ks[4], (Hd, lr)), 'Wgk2': w(ks[5], (lr, key_dim)), 'bgk2': jnp.zeros((key_dim,), dtype=jnp.float32), 'Wg': w(ks[6], (Hd, value_dim)), 'g_norm_weight': jnp.ones((HEAD_V,), dtype=jnp.float32), 'Wo': w(ks[7], (value_dim, Hd))}
    _L1_attn_in = _L1_attn_setup()

    def _L1_ffn_setup():
        import jax, jax.numpy as jnp
        import numpy as np
        TOP_K = 4
        key = jax.random.key(seed)
        ks = jax.random.split(key, 5)
        H, I, E = (256, 96, 32)
        s = 0.02
        return {'hidden_states': jax.random.normal(ks[0], (1, 128, H), jnp.float32), 'router_w': jax.random.normal(ks[1], (E, H), jnp.float32) * s, 'gate_w': jax.random.normal(ks[2], (E, I, H), jnp.float32) * s, 'up_w': jax.random.normal(ks[3], (E, I, H), jnp.float32) * s, 'down_w': jax.random.normal(ks[4], (E, H, I), jnp.float32) * s}
    _L1_ffn_in = _L1_ffn_setup()
    _d = {'L0_attn_x': _L0_attn_in['x'], 'L0_attn_in_proj_w': _L0_attn_in['in_proj_w'], 'L0_attn_conv_w': _L0_attn_in['conv_w'], 'L0_attn_conv_b': _L0_attn_in['conv_b'], 'L0_attn_x_proj_w': _L0_attn_in['x_proj_w'], 'L0_attn_dt_proj_w': _L0_attn_in['dt_proj_w'], 'L0_attn_dt_proj_b': _L0_attn_in['dt_proj_b'], 'L0_attn_out_proj_w': _L0_attn_in['out_proj_w'], 'L0_attn_A_log': _L0_attn_in['A_log'], 'L0_attn_D_param': _L0_attn_in['D_param'], 'L0_ffn_ln1_w': _L0_ffn_in['ln1_w'], 'L0_ffn_ln2_w': _L0_ffn_in['ln2_w'], 'L0_ffn_Wq': _L0_ffn_in['Wq'], 'L0_ffn_Wk': _L0_ffn_in['Wk'], 'L0_ffn_Wv': _L0_ffn_in['Wv'], 'L0_ffn_Wo': _L0_ffn_in['Wo'], 'L0_ffn_A': _L0_ffn_in['A'], 'L0_ffn_B': _L0_ffn_in['B'], 'L0_ffn_W_in_base': _L0_ffn_in['W_in_base'], 'L0_ffn_W_up_base': _L0_ffn_in['W_up_base'], 'L0_ffn_W_down': _L0_ffn_in['W_down'], 'L1_attn_Wq': _L1_attn_in['Wq'], 'L1_attn_Wk': _L1_attn_in['Wk'], 'L1_attn_Wv': _L1_attn_in['Wv'], 'L1_attn_Wgk1': _L1_attn_in['Wgk1'], 'L1_attn_Wgk2': _L1_attn_in['Wgk2'], 'L1_attn_bgk2': _L1_attn_in['bgk2'], 'L1_attn_Wg': _L1_attn_in['Wg'], 'L1_attn_g_norm_weight': _L1_attn_in['g_norm_weight'], 'L1_attn_Wo': _L1_attn_in['Wo'], 'L1_ffn_router_w': _L1_ffn_in['router_w'], 'L1_ffn_gate_w': _L1_ffn_in['gate_w'], 'L1_ffn_up_w': _L1_ffn_in['up_w'], 'L1_ffn_down_w': _L1_ffn_in['down_w']}
    _x0 = _d['L0_attn_x']
    _d['L0_attn_x'] = jax.random.normal(jax.random.fold_in(jax.random.key(seed), 1), (8, 512, 256), dtype=_x0.dtype)
    del _x0
    return _d

def reference(L0_attn_x, L0_attn_in_proj_w, L0_attn_conv_w, L0_attn_conv_b, L0_attn_x_proj_w, L0_attn_dt_proj_w, L0_attn_dt_proj_b, L0_attn_out_proj_w, L0_attn_A_log, L0_attn_D_param, L0_ffn_ln1_w, L0_ffn_ln2_w, L0_ffn_Wq, L0_ffn_Wk, L0_ffn_Wv, L0_ffn_Wo, L0_ffn_A, L0_ffn_B, L0_ffn_W_in_base, L0_ffn_W_up_base, L0_ffn_W_down, L1_attn_Wq, L1_attn_Wk, L1_attn_Wv, L1_attn_Wgk1, L1_attn_Wgk2, L1_attn_bgk2, L1_attn_Wg, L1_attn_g_norm_weight, L1_attn_Wo, L1_ffn_router_w, L1_ffn_gate_w, L1_ffn_up_w, L1_ffn_down_w):

    def _L0_attn_ref(x, in_proj_w, conv_w, conv_b, x_proj_w, dt_proj_w, dt_proj_b, out_proj_w, A_log, D_param):
        import jax, jax.numpy as jnp
        import numpy as np
        BATCH, SEQ, HID, INTER, NSTATE, DTRANK, KCONV = (1, 128, 256, 512, 16, 128, 4)
        EPS = 1e-06

        def _rms(x):
            x32 = x.astype(jnp.float32)
            return (x32 * jax.lax.rsqrt(jnp.mean(x32 * x32, axis=-1, keepdims=True) + EPS)).astype(x.dtype)
        Bsz, L, _ = x.shape
        proj = x @ in_proj_w
        hidden, gate = jnp.split(proj, 2, axis=-1)
        h = jnp.swapaxes(hidden, 1, 2)
        h = jax.lax.conv_general_dilated(h, conv_w, window_strides=(1,), padding=((KCONV - 1, KCONV - 1),), feature_group_count=INTER)[..., :L]
        h = h + conv_b[None, :, None]
        hs = jnp.swapaxes(jax.nn.silu(h), 1, 2)
        ssm_p = hs @ x_proj_w
        dt, Bm, Cm = jnp.split(ssm_p, [DTRANK, DTRANK + NSTATE], axis=-1)
        Bm, Cm, dt = (_rms(Bm), _rms(Cm), _rms(dt))
        dt = jax.nn.softplus(dt @ dt_proj_w + dt_proj_b)
        A = -jnp.exp(A_log.astype(jnp.float32))
        dt32 = dt.astype(jnp.float32)
        u = hs.astype(jnp.float32)
        dA = jnp.exp(dt32[..., None] * A)
        dBu = (dt32 * u)[..., None] * Bm.astype(jnp.float32)[:, :, None, :]
        C32 = Cm.astype(jnp.float32)

        def step(s, inp):
            dA_t, dBu_t, C_t = inp
            s = dA_t * s + dBu_t
            y = jnp.einsum('bdn,bn->bd', s, C_t)
            return (s, y)
        s0 = jnp.zeros((Bsz, INTER, NSTATE), jnp.float32)
        _, ys = jax.lax.scan(step, s0, (jnp.swapaxes(dA, 0, 1), jnp.swapaxes(dBu, 0, 1), jnp.swapaxes(C32, 0, 1)))
        y = jnp.swapaxes(ys, 0, 1)
        y = y + u * D_param
        y = y * jax.nn.silu(gate)
        return y.astype(x.dtype) @ out_proj_w

    def _L0_ffn_ref(hidden_states, ln1_w, ln2_w, Wq, Wk, Wv, Wo, A, B, W_in_base, W_up_base, W_down):
        import jax, jax.numpy as jnp
        import numpy as np
        B_, S, D = (2, 256, 256)
        F_ = 1024
        R = 16
        H = 16
        HD = D // H
        MOD_SCALE = 0.1
        EPS = 1e-06

        def _rmsnorm(x, w):
            v = jnp.mean(x * x, axis=-1, keepdims=True)
            return x * jax.lax.rsqrt(v + EPS) * w

        def _attention(x, Wq, Wk, Wv, Wo):
            b, s, d = x.shape
            q = (x @ Wq.T).reshape(b, s, H, HD)
            k = (x @ Wk.T).reshape(b, s, H, HD)
            v = (x @ Wv.T).reshape(b, s, H, HD)
            scores = jnp.einsum('bqhd,bkhd->bhqk', q, k) / np.sqrt(HD).astype(np.float32)
            causal = jnp.tril(jnp.ones((s, s), bool))
            scores = jnp.where(causal, scores, jnp.finfo(scores.dtype).min)
            probs = jax.nn.softmax(scores, axis=-1)
            out = jnp.einsum('bhqk,bkhd->bqhd', probs, v).reshape(b, s, d)
            return out @ Wo.T
        residual = hidden_states
        x = _rmsnorm(hidden_states, ln1_w)
        attn = _attention(x, Wq, Wk, Wv, Wo)
        mod = MOD_SCALE * jnp.tanh(attn @ A)
        h = _rmsnorm(residual, ln2_w)
        gate_pre = h @ W_in_base.T + mod * (h @ A) @ B
        gate = jax.nn.silu(gate_pre)
        up = h @ W_up_base.T
        mlp_out = gate * up @ W_down.T
        return residual + mlp_out

    def _L1_attn_ref(hidden_states, Wq, Wk, Wv, Wgk1, Wgk2, bgk2, Wg, g_norm_weight, Wo):
        import jax, jax.numpy as jnp
        import numpy as np
        NUM_HEADS = 4
        HEAD_K = 32
        HEAD_V = 64
        CHUNK = 64
        GATE_NORMALIZER = 16.0
        EPS = 1e-05

        def _gla_chunk(q, k, v, gk):
            B, H, S, Dk = q.shape
            Dv = v.shape[-1]
            N = S // CHUNK
            scale = Dk ** (-0.5)

            def to_chunks(x):
                return x.reshape(B, H, N, CHUNK, x.shape[-1]).transpose(2, 0, 1, 3, 4)
            qc, kc, vc, gkc = map(to_chunks, (q, k, v, gk))
            gc = jnp.cumsum(gkc, axis=-2)
            tri = jnp.tril(jnp.ones((CHUNK, CHUNK), dtype=q.dtype))

            def step(Sstate, xs):
                qi, ki, vi, gi = xs
                q_g = qi * jnp.exp(gi) * scale
                k_g = ki * jnp.exp(-gi)
                A = jnp.einsum('bhid,bhjd->bhij', q_g, k_g) * tri
                o_intra = jnp.einsum('bhij,bhjе->bhiе'.replace('е', 'e'), A, vi)
                o_inter = jnp.einsum('bhcd,bhde->bhce', q_g, Sstate)
                g_last = gi[:, :, -1, :]
                k_dec = ki * jnp.exp(g_last[:, :, None, :] - gi)
                S_new = Sstate * jnp.exp(g_last)[..., None] + jnp.einsum('bhcd,bhce->bhde', k_dec, vi)
                return (S_new, o_intra + o_inter)
            S0 = jnp.zeros((B, H, Dk, Dv), dtype=q.dtype)
            _, o = jax.lax.scan(step, S0, (qc, kc, vc, gc))
            return o.transpose(1, 2, 0, 3, 4).reshape(B, H, S, Dv)
        B, S, Hd = hidden_states.shape
        x = hidden_states
        q = (x @ Wq).reshape(B, S, NUM_HEADS, HEAD_K).transpose(0, 2, 1, 3)
        k = (x @ Wk).reshape(B, S, NUM_HEADS, HEAD_K).transpose(0, 2, 1, 3)
        v = (x @ Wv).reshape(B, S, NUM_HEADS, HEAD_V).transpose(0, 2, 1, 3)
        gk = x @ Wgk1 @ Wgk2 + bgk2
        gk = jax.nn.log_sigmoid(gk) / GATE_NORMALIZER
        gk = gk.reshape(B, S, NUM_HEADS, HEAD_K).transpose(0, 2, 1, 3)
        o = _gla_chunk(q, k, v, gk)
        o = o.transpose(0, 2, 1, 3)
        g = (x @ Wg).reshape(B, S, NUM_HEADS, HEAD_V)
        rms = jnp.sqrt(jnp.mean(o * o, axis=-1, keepdims=True) + EPS)
        o = o / rms * g_norm_weight * (g * jax.nn.sigmoid(g))
        o = o.reshape(B, S, NUM_HEADS * HEAD_V)
        return o @ Wo

    def _L1_ffn_ref(hidden_states, router_w, gate_w, up_w, down_w):
        import jax, jax.numpy as jnp
        import numpy as np
        TOP_K = 4
        B, S, H = hidden_states.shape
        E = router_w.shape[0]
        x = hidden_states.reshape(-1, H)
        logits = x @ router_w.T
        probs = jax.nn.softmax(logits.astype(jnp.float32), axis=-1)
        rw, sel = jax.lax.top_k(probs, TOP_K)
        rw = rw / jnp.sum(rw, axis=-1, keepdims=True)
        rw = rw.astype(x.dtype)

        def body(acc, expert):
            gw, uw, dw, e = expert
            w_tok = jnp.sum(jnp.where(sel == e, rw, 0.0), axis=-1)
            h = jax.nn.silu(x @ gw.T) * (x @ uw.T)
            y = h @ dw.T
            return (acc + w_tok[:, None] * y, None)
        acc0 = jnp.zeros_like(x)
        out, _ = jax.lax.scan(body, acc0, (gate_w, up_w, down_w, jnp.arange(E)))
        return out.reshape(B, S, H)
    x = L0_attn_x
    x = x + _L0_attn_ref(_layernorm(x, axis=-1), L0_attn_in_proj_w, L0_attn_conv_w, L0_attn_conv_b, L0_attn_x_proj_w, L0_attn_dt_proj_w, L0_attn_dt_proj_b, L0_attn_out_proj_w, L0_attn_A_log, L0_attn_D_param)
    x = x + _L0_ffn_ref(_layernorm(x, axis=-1), L0_ffn_ln1_w, L0_ffn_ln2_w, L0_ffn_Wq, L0_ffn_Wk, L0_ffn_Wv, L0_ffn_Wo, L0_ffn_A, L0_ffn_B, L0_ffn_W_in_base, L0_ffn_W_up_base, L0_ffn_W_down)
    x = x + _L1_attn_ref(_layernorm(x, axis=-1), L1_attn_Wq, L1_attn_Wk, L1_attn_Wv, L1_attn_Wgk1, L1_attn_Wgk2, L1_attn_bgk2, L1_attn_Wg, L1_attn_g_norm_weight, L1_attn_Wo)
    x = x + _L1_ffn_ref(_layernorm(x, axis=-1), L1_ffn_router_w, L1_ffn_gate_w, L1_ffn_up_w, L1_ffn_down_w)
    return x

_drawn_inputs = setup_inputs


def setup_inputs(seed=0):
    import zlib

    import numpy as np

    out = dict(_drawn_inputs(seed))
    spreads = {'L0_attn_conv_b': (0.0, 0.365),
     'L0_attn_D_param': (1.0, 0.6),
     'L0_ffn_ln1_w': (1.0, 0.6),
     'L0_ffn_ln2_w': (1.0, 0.6),
     'L1_attn_bgk2': (0.0, 2.0),
     'L1_attn_g_norm_weight': (1.0, 0.6)}
    factors = {'L0_attn_dt_proj_w': 4.614,
     'L0_attn_dt_proj_b': 8.0,
     'L0_attn_A_log': 8.0,
     'L0_ffn_Wq': 64.0,
     'L0_ffn_Wk': 64.0,
     'L0_ffn_Wv': 64.0,
     'L0_ffn_Wo': 64.0,
     'L0_ffn_A': 64.0,
     'L0_ffn_B': 64.0,
     'L0_ffn_W_in_base': 3.011,
     'L0_ffn_W_up_base': 2.975,
     'L0_ffn_W_down': 2.977,
     'L1_attn_Wgk1': 32.053,
     'L1_attn_Wgk2': 23.986,
     'L1_ffn_router_w': 8.0,
     'L1_ffn_gate_w': 8.0,
     'L1_ffn_up_w': 8.0,
     'L1_ffn_down_w': 8.0}
    for name, (base, spread) in spreads.items():
        noise = np.random.default_rng([zlib.crc32(name.encode()), seed]).standard_normal(out[name].shape)
        drawn = base * np.exp(spread * noise) if base else spread * noise
        out[name] = jnp.asarray(drawn.astype(out[name].dtype))
    for name, factor in factors.items():
        out[name] = (out[name] * factor).astype(out[name].dtype)
    return out
```

```python
from contextlib import ExitStack

import numpy as np
import concourse.bass as bass
from concourse import mybir

F32 = mybir.dt.float32
BF16 = mybir.dt.bfloat16
ALU = mybir.AluOpType
ACT = mybir.ActivationFunctionType
AX = mybir.AxisListType

P = 128
BATCH, SEQ, HID = 8, 512, 256
NT = SEQ // P
NF = HID // P
INTER, NSTATE, DTRANK, KCONV = 512, 16, 128, 4
NCT = INTER // P
NSSM = DTRANK + 2 * NSTATE
HEADS, HD, RANK, FFN = 16, 16, 16, 1024
HPT = 4
NQT = HEADS // HPT
GH, GK, GV, CHUNK = 4, 32, 64, 64
NCHUNK = SEQ // CHUNK
GHK, GHV = GH * GK, GH * GV
EXPERTS, EI, TOPK = 32, 96, 4
NFT = FFN // P
NMT = EXPERTS * EI // P
NWT = NFT + NMT
WT = 2 * NF * P + HID
MASKED = -3.0e38

RESIDENT = [
    ("m_in", NF * 2 * INTER), ("m_x", NCT * NSSM), ("m_dt", INTER), ("m_out", NCT * HID),
    ("conv_w", NCT * KCONV), ("conv_b", NCT), ("dt_b", NCT), ("a_log", NCT * NSTATE), ("skip", NCT),
    ("ln1", NF), ("ln2", NF),
    ("wq", NF * NQT * P), ("wk", NF * NQT * P), ("wv", NF * HID), ("mod_a", NF * RANK),
    ("g_q", NF * GHK), ("g_k", NF * GHK), ("g_v", NF * GHV), ("g_g", NF * GHV), ("g_gk1", NF * RANK),
    ("g_bias", 1), ("g_o", NF * HID), ("router", NF * EXPERTS),
]
OFFSET = {}
_at = 0
for _name, _n in RESIDENT:
    OFFSET[_name] = (_at, _n)
    _at += _n
RES = _at


class Signal:

    def __init__(self, sem, per, primed=False):
        self.sem, self.per, self.primed = sem, per, primed

    def at(self, turn, k):
        return (turn + 1) * self.per + k if self.primed else turn * self.per + k


class Steps(Signal):

    def __init__(self, sem, name, counted):
        super().__init__(sem, counted.get(name, 1))
        self.n, self.name, self.counted = 0, name, counted

    def step(self, instruction):
        self.n += 1
        return self.n

    def named(self, turn, name):
        return self.at(turn, self.counted.get(name, 1))


class Ring:

    def __init__(self, sem, name, banks, jobs):
        self.banks, self.jobs = banks, jobs
        self.index = {key: j for j, (key, _) in enumerate(jobs)}
        self.ready = Signal(sem(name + "_ready"), len(jobs))
        self.freed = {}
        for e in ("act", "dve"):
            n = sum(1 for _, c in jobs if c == e)
            if n:
                self.freed[e] = Signal(sem(f"{name}_freed_{e}"), n, primed=True)
        self.count, seen = [], {"act": 0, "dve": 0}
        for _, e in jobs:
            seen[e] += 1
            self.count.append(seen[e])

    def bank(self, key):
        return self.banks[self.index[key] % len(self.banks)]

    def filled_at(self, turn, key):
        return self.ready.at(turn, self.index[key] + 1)

    def freed_sem(self, key):
        return self.freed[self.jobs[self.index[key]][1]].sem

    def freed_at(self, turn, key):
        j = self.index[key]
        return self.freed[self.jobs[j][1]].at(turn, self.count[j])

    def before(self, key):
        j, n = self.index[key], len(self.banks)
        if j >= n:
            return j - n, False
        return max(i for i in range(len(self.jobs)) if i % n == j), True

    def last_sem(self, key):
        return self.freed[self.jobs[self.before(key)[0]][1]].sem

    def last_at(self, turn, key):
        j, earlier = self.before(key)
        signal = self.freed[self.jobs[j][1]]
        return signal.at(turn, self.count[j] - (signal.per if earlier else 0))


def rest_jobs():
    jobs = [("zT", c, "act") for c in range(NF)]
    jobs += [("q", i, "act") for i in range(NQT)] + [("k", i, "dve") for i in range(NQT)]
    jobs += [("v", i, "dve") for i in range(2)]
    n = NT * HEADS
    for i in range(n + 2):
        if i < n:
            jobs.append(("S", i, "act"))
        if i >= 2:
            jobs.append(("PT", i - 2, ("act", "dve")[i % 2]))
    jobs += [("oT", c, "act") for c in range(NF)] + [("mod", 0, "act"), ("hA", 0, "dve")]
    for f in range(NFT):
        jobs += [("gate", f, "act"), ("up", f, "dve")]
    jobs += [("nT", c, "act") for c in range(NF)]
    jobs += [("low", 0, "act"), ("gk", 0, "act"), ("gq", 0, "act"), ("gkey", 0, "act")]
    jobs += [("gv", i, "dve") for i in range(2)] + [("gg", i, "act") for i in range(2)]
    jobs += [("kdT", 0, "act")]
    jobs += [("dS", c, "dve") for c in range(NCHUNK - 1)] + [("AT", t, "dve") for t in range(NT)]
    jobs += [("GO", t, "act") for t in range(NT)] + [("goT", c, "act") for c in range(NF)]
    jobs += [("gout", i, "dve") for i in range(2)]
    jobs += [("mT", c, "act") for c in range(NF)] + [("rt", 0, "dve"), ("wT", 0, "act")]
    for f in range(NFT, NWT):
        jobs += [("gate", f, "act"), ("up", f, "dve"), ("share", f, "dve")]
    return [((name, i), e) for name, i, e in jobs]


def scan_jobs():
    jobs = [("T", c, "act") for c in range(NF)] + [("hid", c, "act") for c in range(NCT)]
    jobs += [("gate", c, "act") for c in range(NCT)] + [("ssm", i, "act") for i in range(2)]
    jobs += [("dtT", 0, "act"), ("bcT", 0, "act")] + [("dtp", c, "act") for c in range(NCT)]
    jobs += [("out", i, "dve") for i in range(2)]
    return [((name, i), e) for name, i, e in jobs]


def build(nc, counted, x, w, wt, mod_b, wo, g_gk2, g_norm, out):
    with ExitStack() as ctx:
        used = [0]

        def sb(name, floats, dt=F32, parts=P):
            used[0] += floats * (2 if dt == BF16 else 4)
            return ctx.enter_context(nc.sbuf_tensor(name, [parts, floats], dt))

        def sem(name):
            return ctx.enter_context(nc.semaphore(name))

        res = sb("resident", RES)

        def weight(name):
            at, n = OFFSET[name]
            return res[:, at:at + n]

        m_in = weight("m_in").rearrange("p (c n) -> p c n", c=NF)
        m_x = weight("m_x").rearrange("p (c n) -> p c n", c=NCT)
        m_dt = weight("m_dt")
        m_out = weight("m_out").rearrange("p (c n) -> p c n", c=NCT)
        conv_w = weight("conv_w").rearrange("p (c k) -> p c k", c=NCT)
        conv_b, dt_b, skip = weight("conv_b"), weight("dt_b"), weight("skip")
        a_neg = weight("a_log").rearrange("p (c n) -> p c n", c=NCT)
        ln1, ln2 = weight("ln1"), weight("ln2")
        wq = weight("wq").rearrange("p (c n) -> p c n", c=NF)
        wk = weight("wk").rearrange("p (c n) -> p c n", c=NF)
        wv = weight("wv").rearrange("p (c n) -> p c n", c=NF)
        mod_a = weight("mod_a").rearrange("p (c n) -> p c n", c=NF)
        g_q = weight("g_q").rearrange("p (c n) -> p c n", c=NF)
        g_k = weight("g_k").rearrange("p (c n) -> p c n", c=NF)
        g_v = weight("g_v").rearrange("p (c n) -> p c n", c=NF)
        g_g = weight("g_g").rearrange("p (c n) -> p c n", c=NF)
        g_gk1 = weight("g_gk1").rearrange("p (c n) -> p c n", c=NF)
        g_bias = weight("g_bias")
        g_o = weight("g_o").rearrange("p (c n) -> p c n", c=NF)
        router = weight("router").rearrange("p (c n) -> p c n", c=NF)
        modb = sb("modb", FFN, parts=RANK)
        gk2 = sb("gk2", GHK, parts=RANK)
        gnorm = sb("gnorm", GV)
        wo_a = sb("wo_a", NF * RANK)[:, :].rearrange("p (c r) -> p c r", c=NF)
        ident = sb("ident", P)
        ident_b = sb("ident_b", P, BF16)
        causal = sb("causal", P, BF16)
        tri = sb("tri", GH * CHUNK)
        blockdiag = sb("blockdiag", GHV)
        chunk_starts = sb("chunk_starts", SEQ)
        expert_starts = sb("expert_starts", NT * EXPERTS)
        select = sb("select", NMT * P, BF16, parts=3 * EXPERTS)
        minus_half = sb("minus_half", 16)
        g_nbias = sb("g_nbias", 1)

        xa = sb("xa", NT * HID)[:, :].rearrange("p (t d) -> p t d", t=NT)
        xnT = sb("xnT", NF * SEQ)[:, :].rearrange("p (c t) -> p c t", c=NF)
        hid_dtu = sb("hid_dtu", NCT * (SEQ + KCONV - 1))
        hid = hid_dtu[:, :].rearrange("p (c t) -> p c t", c=NCT)
        dtu = hid_dtu[:, 0:NCT * SEQ].rearrange("p (c t) -> p c t", c=NCT)
        sgate = sb("sgate", NCT * SEQ)[:, :].rearrange("p (c t) -> p c t", c=NCT)
        u = sb("u", NCT * SEQ)[:, :].rearrange("p (c t) -> p c t", c=NCT)
        dt = sb("dt", NCT * SEQ)[:, :].rearrange("p (c t) -> p c t", c=NCT)
        yacc = sb("yacc", NCT * SEQ)[:, :].rearrange("p (c t) -> p c t", c=NCT)
        decay_all = sb("decay", 4 * SEQ)
        drive_all = sb("drive", 4 * SEQ)
        decay = decay_all[:, :].rearrange("p (b n t) -> p b n t", b=2, n=2)
        drive = drive_all[:, :].rearrange("p (b n t) -> p b n t", b=2, n=2)
        bc = sb("bc", 8 * SEQ)[:, :].rearrange("p (b g n t) -> p b g n t", b=2, g=2, n=2)
        dtnT = sb("dtnT", SEQ)
        bcT = sb("bcT", SEQ, parts=2 * NSTATE)
        xn = drive_all[:, 0:NT * HID].rearrange("p (t d) -> p t d", t=NT)
        ssm = decay_all[:, 0:NT * NSSM].rearrange("p (t n) -> p t n", t=NT)
        ssm_sq = drive_all[:, 0:NT * NSSM].rearrange("p (t n) -> p t n", t=NT)
        sp_exp = yacc
        sp_log = decay_all[:, :].rearrange("p (c t) -> p c t", c=NCT)
        sp_relu = drive_all[:, :].rearrange("p (c t) -> p c t", c=NCT)
        a_stats = sb("a_stats", NT * 6)[:, :].rearrange("p (t n) -> p t n", t=NT)
        a_mv = sb("a_mv", NT * 2)[:, :].rearrange("p (t n) -> p t n", t=NT)
        a_rs = sb("a_rs", NT)
        a_ss = sb("a_ss", 3 * NT)

        xb = sb("xb", NT * HID)[:, :].rearrange("p (t d) -> p t d", t=NT)
        n_all = sb("n_all", NT * HID)
        nrm = n_all[:, :].rearrange("p (t d) -> p t d", t=NT)
        xT = sb("xT", NF * SEQ)[:, :].rearrange("p (c t) -> p c t", c=NF)
        hT_all = sb("hT", NF * SEQ)
        hT = hT_all[:, :].rearrange("p (c t) -> p c t", c=NF)
        NSLOT = 3
        wslot = sb("wslot", NSLOT * WT)[:, :].rearrange("p (s n) -> p s n", s=NSLOT)
        R = sb("rest", 20 * SEQ)

        def area(first, n, count=1):
            return R[:, first * SEQ:first * SEQ + n * count]

        qT = area(0, SEQ, NQT).rearrange("p (c t) -> p c t", c=NQT)
        kT = area(4, SEQ, NQT).rearrange("p (c t) -> p c t", c=NQT)
        v = area(8, HID, NT).rearrange("p (t d) -> p t d", t=NT)
        NPS = 3
        prob = area(10, SEQ, NPS).rearrange("p (s t) -> p s t", s=NPS)
        probT = area(13, SEQ, NPS).rearrange("p (s t) -> p s t", s=NPS)
        gmod = area(16, SEQ)[0:RANK, :]
        tanhT = area(17, SEQ)[0:RANK, :]
        o_tok = nrm
        oT = xT
        act_gate = area(0, SEQ, 2).rearrange("p (s t) -> p s t", s=2)
        inner = area(2, SEQ, 2).rearrange("p (s t) -> p s t", s=2)
        gq = area(4, SEQ)
        gkey = area(5, SEQ)
        kg = area(6, SEQ)
        cs = area(7, SEQ)
        e_q, e_kg, e_kd = area(8, SEQ), area(9, SEQ), area(10, SEQ)
        at_m = area(8, GH * CHUNK, NT).rearrange("p (t n) -> p t n", t=NT)
        qbd = area(11, SEQ, 4).rearrange("p (c h i) -> p c h i", c=NCHUNK, h=GH)
        gv = area(15, GHV, NT).rearrange("p (t n) -> p t n", t=NT)
        gg = area(17, GHV, NT).rearrange("p (t n) -> p t n", t=NT)
        kd_tok = area(19, SEQ).rearrange("p (t n) -> p t n", t=NT)
        g_abs, g_relu, g_log, lowT = (area(i, SEQ) for i in range(4))
        state = R[:, 0:NCHUNK * GHV].rearrange("p (c n) -> p c n", c=NCHUNK)
        go = nrm
        go_sq = hT_all[:, :].rearrange("p (t n) -> p t n", t=NT)
        goT = xT
        g_last = sb("g_last", NCHUNK)
        share = hT_all[0:3 * EXPERTS, 0:SEQ // 2].bitcast(BF16)
        shareT = hT_all[0:EXPERTS, SEQ // 2:SEQ // 2 + SEQ]
        share_mid = hT_all[0:EXPERTS, 3 * SEQ // 2:2 * SEQ].bitcast(BF16)
        NE = NT * EXPERTS
        rt = {n: area(4, SEQ, 4)[:, i * NE:(i + 1) * NE] for i, n in
              enumerate(("e", "gt", "eq", "pre", "sel", "lm"))}
        stats = sb("stats", NT * 6)[:, :].rearrange("p (t n) -> p t n", t=NT)
        mv = sb("mv", NT * 2)[:, :].rearrange("p (t n) -> p t n", t=NT)
        rs, rs2 = sb("rs", NT), sb("rs2", NT)
        neg_max, prob_sum = sb("neg_max", NT * HEADS), sb("prob_sum", NT * HEADS)
        g_ss = sb("g_ss", NT * GH)
        small = sb("small", 16 * NT)

        bank = [ctx.enter_context(nc.psum_tensor(f"bank{i}", [P, 512], F32)) for i in range(8)]
        A = Ring(sem, "scan_bank", bank[0:2], scan_jobs())
        B = Ring(sem, "rest_bank", bank[2:6], rest_jobs())
        D = bank[6:8]
        d_free = Signal(sem("d_free"), NT + 2, primed=True)

        weights_in = sem("weights_in")
        consts = sem("consts")
        const_steps = sem("const_steps")
        prep = sem("prep")
        x_in = Signal(sem("x_in"), 16)
        xa_free = Signal(sem("xa_free"), 1, primed=True)
        bc_out = Signal(sem("bc_out"), 16)
        bc_in = [Signal(sem(f"bc_in{i}"), 16 * NSTATE // 4) for i in range(2)]
        pair_used = Signal(sem("pair_used"), NSTATE // 2, primed=True)
        NU = NSTATE // 2 * NCT
        decay_ready = Signal(sem("decay_ready"), NU)
        decay_used = Signal(sem("decay_used"), NU)
        unit_done = Signal(sem("unit_done"), NU)
        unit_added = Signal(sem("unit_added"), NU)
        w_in = [Signal(sem(f"w_in{i}"), 16 * len(range(i, NWT, NSLOT))) for i in range(NSLOT)]
        down_done = Signal(sem("down_done"), NWT, primed=True)
        inner_ready = Signal(sem("inner_ready"), NWT, primed=True)
        pv_done = Signal(sem("pv_done"), NT * HEADS)
        max_ready = Signal(sem("max_ready"), NT * HEADS)
        out_stored = Signal(sem("out_stored"), 16, primed=True)
        sv = Steps(sem("scan_dve_steps"), "scan_v", counted)
        sp_ = Steps(sem("scan_pool_steps"), "scan_p", counted)
        sa = Steps(sem("scan_act_steps"), "scan_a", counted)
        rv = Steps(sem("rest_dve_steps"), "rest_v", counted)
        rp = Steps(sem("rest_pool_steps"), "rest_p", counted)
        ra = Steps(sem("rest_act_steps"), "rest_a", counted)
        mark = {}

        bc_dram = nc.dram_tensor("bc_dram", [2 * NSTATE, SEQ], F32).ap()

        def marked(name, k):
            mark[name] = k
            return k

        passed = sem("passed")

        def apart(eng):
            eng.sem_inc(passed, 1)

        block = ctx.enter_context(nc.Block())

        @block.sync
        def _(sp):
            sp.sem_inc(out_stored.sem, out_stored.per)
            sp.dma_start(res[:, :], w).then_inc(weights_in, 16)
            sp.dma_start(modb[:, :], mod_b).then_inc(weights_in, 16)
            sp.dma_start(gk2[:, :], g_gk2).then_inc(weights_in, 16)
            sp.dma_start(gnorm[:, :], g_norm.partition_broadcast(P)).then_inc(weights_in, 16)
            sp.dma_start(area(0, SEQ).rearrange("p (c n) -> p c n", c=NF),
                         wo.rearrange("(c p) n -> p c n", p=P)).then_inc(weights_in, 16)

            def scan_in(turn):
                sp.wait_ge(xa_free.sem, xa_free.at(turn, 0))
                sp.dma_start(xa, x[bass.ds(turn, 1)].rearrange("b (t p) d -> p (b t) d", p=P)).then_inc(x_in.sem, 16)
                sp.wait_ge(A.freed_sem(("bcT", 0)), A.freed_at(turn, ("bcT", 0)))
                sp.dma_start(bc_dram, bcT[:, :]).then_inc(bc_out.sem, 16)
                sp.wait_ge(bc_out.sem, bc_out.at(turn, 16))
                for pair in range(NSTATE // 2):
                    sp.wait_ge(pair_used.sem, pair_used.at(turn, pair - 1))
                    rows = bc_dram.rearrange("(g n) t -> g n t", g=2)[:, 2 * pair:2 * pair + 2, :]
                    sp.dma_start(bc[:, pair % 2], rows.partition_broadcast(P)).then_inc(bc_in[pair % 2].sem, 16)

            def rest_io(turn):
                for f in range(NWT):
                    sp.wait_ge(down_done.sem, down_done.at(turn, f - NSLOT + 1 if f >= NSLOT else max(g for g in range(NWT) if g % NSLOT == f) + 1 - NWT))
                    sp.dma_start(wslot[:, f % NSLOT, :], wt[f]).then_inc(w_in[f % NSLOT].sem, 16)
                sp.wait_ge(rv.sem, rv.named(turn, "x_out"))
                sp.dma_start(out[bass.ds(turn, 1)].rearrange("b (t p) d -> p (b t) d", p=P), xb).then_inc(out_stored.sem, 16)

            with sp.Fori(0, BATCH) as turn:
                scan_in(turn)
                rest_io(turn)
            sp.wait_ge(out_stored.sem, out_stored.at(BATCH - 1, 16))

        @block.gpsimd
        def _(pool):
            g = nc.gpsimd
            k = [0]

            def const(ins):
                k[0] += 1
                ins.then_inc(const_steps, 1)
                pool.wait_ge(const_steps, k[0])

            const(g.memset(ident[:, :], 0.0))
            const(g.affine_select(out=ident[:, :], in_=ident[:, :], compare_op=ALU.not_equal, fill=1.0,
                                  base=0, pattern=[[-1, P]], channel_multiplier=1))
            const(g.tensor_copy(ident_b[:, :], ident[:, :]))
            const(g.memset(causal[:, :], 0.0))
            const(g.affine_select(out=causal[:, :], in_=causal[:, :], compare_op=ALU.is_ge, fill=MASKED,
                                  base=0, pattern=[[-1, P]], channel_multiplier=1))
            const(g.memset(tri[:, :], 1.0))
            for half in range(2):
                part = tri[half * CHUNK:(half + 1) * CHUNK, :].rearrange("p (h i) -> p h i", h=GH)
                const(g.affine_select(out=part, in_=part, compare_op=ALU.is_ge, fill=0.0, base=0,
                                      pattern=[[0, GH], [1, CHUNK]], channel_multiplier=-1))
            const(g.memset(blockdiag[:, :], 0.0))
            for h in range(GH):
                const(g.memset(blockdiag[h * GK:(h + 1) * GK, h * GV:(h + 1) * GV], 1.0))
            const(g.memset(chunk_starts[:, :], 1.0))
            const(g.memset(chunk_starts[:, 0:SEQ:CHUNK], 0.0))
            const(g.memset(expert_starts[:, :], 1.0))
            const(g.memset(expert_starts[:, 0:NE:EXPERTS], 0.0))
            const(g.memset(select[:, :], 0.0))
            for part in range(3):
                rows = select[part * EXPERTS:(part + 1) * EXPERTS, :].rearrange("p (e i) -> p e i", e=EXPERTS)
                const(g.affine_select(out=rows, in_=rows, compare_op=ALU.not_equal, fill=1.0, base=0,
                                      pattern=[[-1, EXPERTS], [0, EI]], channel_multiplier=1))
            g.memset(minus_half[:, :], -0.5).then_inc(consts, 1)
            pool.wait_ge(consts, 1)

            def power(steps, turn, out_, in_, scale, eps, n):
                s = steps.step(g.tensor_scalar(out_, in_, scale, eps, ALU.mult, ALU.add).then_inc(steps.sem, 1))
                pool.wait_ge(steps.sem, steps.at(turn, s))
                return steps.step(g.tensor_tensor(out_, out_, minus_half[:, 0:n], ALU.pow).then_inc(steps.sem, 1))

            def scan_part(turn):
                pool.wait_ge(sv.sem, sv.named(turn, "a_mv"))
                apart(pool)
                marked("a_rs", power(sp_, turn, a_rs[:, :], a_mv[:, :, 1], 1.0, 1e-5, NT))
                pool.wait_ge(sv.sem, sv.named(turn, "a_ss"))
                apart(pool)
                s = sp_.step(g.tensor_scalar(a_ss[:, 0:NT], a_ss[:, 0:NT], 1.0 / DTRANK, 1e-6, ALU.mult, ALU.add).then_inc(sp_.sem, 1))
                s = sp_.step(g.tensor_scalar(a_ss[:, NT:3 * NT], a_ss[:, NT:3 * NT], 1.0 / NSTATE, 1e-6, ALU.mult, ALU.add).then_inc(sp_.sem, 1))
                pool.wait_ge(sp_.sem, sp_.at(turn, s))
                marked("a_rr", sp_.step(g.tensor_tensor(a_ss[:, :], a_ss[:, :], minus_half[:, 0:3 * NT], ALU.pow).then_inc(sp_.sem, 1)))
                yield
                for c in range(NCT):
                    pool.wait_ge(sa.sem, sa.named(turn, f"sp_exp{c}"))
                    apart(pool)
                    s1 = sp_.step(g.tensor_scalar(dt[:, c], sp_exp[:, c], 1.0, -1.0, ALU.add, ALU.add).then_inc(sp_.sem, 1))
                    pool.wait_ge(sa.sem, sa.named(turn, f"sp_log{c}"))
                    pool.wait_ge(sp_.sem, sp_.at(turn, s1))
                    s = sp_.step(g.tensor_tensor(dt[:, c], sp_log[:, c], dt[:, c], ALU.subtract).then_inc(sp_.sem, 1))
                    pool.wait_ge(sp_.sem, sp_.at(turn, s))
                    s = sp_.step(g.tensor_tensor(dt[:, c], dt[:, c], sp_exp[:, c], ALU.add).then_inc(sp_.sem, 1))
                    pool.wait_ge(sp_.sem, sp_.at(turn, s))
                    marked(f"dt{c}", sp_.step(g.tensor_tensor(dt[:, c], dt[:, c], sp_relu[:, c], ALU.add).then_inc(sp_.sem, 1)))
                    yield
                pool.wait_ge(sp_.sem, sp_.at(turn, s + 1))
                apart(pool)
                marked("decay_zero", sp_.step(g.memset(decay_all[:, 0:4 * SEQ:SEQ], 0.0).then_inc(sp_.sem, 1)))
                for unit in range(NU):
                    c, slot = unit % NCT, unit % 2
                    pool.wait_ge(unit_done.sem, unit_done.at(turn, unit + 1))
                    if unit < NCT:
                        g.tensor_tensor(yacc[:, c], drive[:, slot, 0], drive[:, slot, 1], ALU.add).then_inc(unit_added.sem, 1)
                    else:
                        s = sp_.step(g.tensor_tensor(drive[:, slot, 0], drive[:, slot, 0], drive[:, slot, 1], ALU.add).then_inc(sp_.sem, 1))
                        pool.wait_ge(sp_.sem, sp_.at(turn, s))
                        g.tensor_tensor(yacc[:, c], yacc[:, c], drive[:, slot, 0], ALU.add).then_inc(unit_added.sem, 1)
                    yield

            def rest_part(turn):
                pool.wait_ge(rv.sem, rv.named(turn, "mv0"))
                apart(pool)
                s = power(rp, turn, rs[:, :], mv[:, :, 1], 1.0, 1e-5, NT)
                marked("rs0", s)
                pool.wait_ge(rp.sem, rp.at(turn, s))
                s = rp.step(g.tensor_tensor(rs2[:, :], rs[:, :], rs[:, :], ALU.mult).then_inc(rp.sem, 1))
                pool.wait_ge(rp.sem, rp.at(turn, s))
                s = rp.step(g.tensor_tensor(rs2[:, :], rs2[:, :], mv[:, :, 1], ALU.mult).then_inc(rp.sem, 1))
                pool.wait_ge(rp.sem, rp.at(turn, s))
                apart(pool)
                marked("rs2", power(rp, turn, rs2[:, :], rs2[:, :], 1.0, 1e-6, NT))
                yield
                pool.wait_ge(rv.sem, rv.named(turn, "mv1"))
                apart(pool)
                marked("rs1", power(rp, turn, rs[:, :], mv[:, :, 1], 1.0, 1e-5, NT))
                pool.wait_ge(rv.sem, rv.named(turn, "att_done"))
                apart(pool)
                marked("qbd0", rp.step(g.memset(R[:, 11 * SEQ:15 * SEQ], 0.0).then_inc(rp.sem, 1)))
                yield
                pool.wait_ge(ra.sem, ra.named(turn, "g_exp"))
                apart(pool)
                s = rp.step(g.tensor_scalar(cs, g_abs, 1.0, -1.0, ALU.add, ALU.add).then_inc(rp.sem, 1))
                pool.wait_ge(ra.sem, ra.named(turn, "g_log"))
                pool.wait_ge(rp.sem, rp.at(turn, s))
                s = rp.step(g.tensor_tensor(cs, g_log, cs, ALU.subtract).then_inc(rp.sem, 1))
                pool.wait_ge(rp.sem, rp.at(turn, s))
                s = rp.step(g.tensor_tensor(cs, cs, g_abs, ALU.add).then_inc(rp.sem, 1))
                pool.wait_ge(rp.sem, rp.at(turn, s))
                marked("g_soft", rp.step(g.tensor_tensor(g_log, cs, g_relu, ALU.add).then_inc(rp.sem, 1)))
                yield
                pool.wait_ge(rv.sem, rv.named(turn, "qg"))
                apart(pool)
                for h in range(GH):
                    rows = slice(h * GK, (h + 1) * GK)
                    s = rp.step(g.tensor_copy(qbd[rows, :, h, :], gq[rows, :].rearrange("p (c i) -> p c i", c=NCHUNK)).then_inc(rp.sem, 1))
                    pool.wait_ge(rp.sem, rp.at(turn, s))
                    apart(pool)
                marked("qbd", s)
                pool.wait_ge(B.freed_sem(("gg", 1)), B.freed_at(turn, ("gg", 1)))
                for t in range(NT):
                    s = rp.step(g.tensor_tensor(gg[:, t].rearrange("p (h n) -> p h n", h=GH), gg[:, t].rearrange("p (h n) -> p h n", h=GH), gnorm[:, :].unsqueeze(1).broadcast_to([P, GH, GV]), ALU.mult).then_inc(rp.sem, 1))
                marked("gg", s)
                yield
                pool.wait_ge(rv.sem, rv.named(turn, "g_ss"))
                apart(pool)
                marked("g_rr", power(rp, turn, g_ss[:, :], g_ss[:, :], 1.0 / GV, 1e-5, NT * GH))
                yield
                pool.wait_ge(rv.sem, rv.named(turn, "mv2"))
                apart(pool)
                marked("rsm", power(rp, turn, rs[:, :], mv[:, :, 1], 1.0, 1e-5, NT))
                yield

            with pool.Fori(0, BATCH) as turn:
                for _ in scan_part(turn):
                    pass
                for _ in rest_part(turn):
                    pass

        @block.scalar
        def _(act):
            a = nc.scalar
            act.sem_inc(A.freed["act"].sem, A.freed["act"].per)
            act.sem_inc(B.freed["act"].sem, B.freed["act"].per)
            act.wait_ge(weights_in, 80)
            a.activation(a_neg, a_neg, ACT.Exp).then_inc(prep, 1)
            act.wait_ge(prep, 1)
            a.activation(a_neg, a_neg, ACT.Copy, scale=-1.0).then_inc(prep, 1)
            a.activation(g_nbias[:, :], g_bias, ACT.Copy, scale=-1.0).then_inc(prep, 1)
            act.wait_ge(prep, 3)

            def empty(ring, turn, key, dst, func=ACT.Copy, src=None, **kw):
                act.wait_ge(ring.ready.sem, ring.filled_at(turn, key))
                b = ring.bank(key)
                a.activation(dst, b[:, :] if src is None else src(b), func, **kw).then_inc(ring.freed_sem(key), 1)

            def scan_part(turn):
                for c in range(NF):
                    empty(A, turn, ("T", c), xnT[:, c])
                for c in range(NCT):
                    empty(A, turn, ("hid", c), hid[:, c, KCONV - 1:])
                    yield
                for c in range(NCT):
                    empty(A, turn, ("gate", c), sgate[:, c], ACT.Silu)
                yield
                for c in range(NCT):
                    act.wait_ge(sv.sem, sv.named(turn, f"conv{c}"))
                    s = sa.step(a.activation(u[:, c], dt[:, c], ACT.Silu, bias=conv_b[:, c:c + 1]).then_inc(sa.sem, 1))
                marked("u", s)
                yield
                for i in range(2):
                    act.wait_ge(A.ready.sem, A.filled_at(turn, ("ssm", i)))
                    b = A.bank(("ssm", i))
                    src = b[:, :].rearrange("p (t n) -> p t n", t=2)[:, :, 0:NSSM]
                    s = sa.step(a.activation(ssm_sq[:, 2 * i:2 * i + 2], src, ACT.Square).then_inc(sa.sem, 1))
                    a.activation(ssm[:, 2 * i:2 * i + 2], src, ACT.Copy).then_inc(A.freed_sem(("ssm", i)), 1)
                marked("ssm_sq", s)
                yield
                empty(A, turn, ("dtT", 0), dtnT[:, :])
                empty(A, turn, ("bcT", 0), bcT[:, :], src=lambda b: b[0:2 * NSTATE, :])
                for c in range(NCT):
                    act.wait_ge(A.ready.sem, A.filled_at(turn, ("dtp", c)))
                    b = A.bank(("dtp", c))
                    s = sa.step(a.activation(sp_exp[:, c], b[:, :], ACT.Abs, bias=dt_b[:, c:c + 1]).then_inc(sa.sem, 1))
                    a.activation(sp_relu[:, c], b[:, :], ACT.Relu, bias=dt_b[:, c:c + 1]).then_inc(A.freed_sem(("dtp", c)), 1)
                    act.wait_ge(sa.sem, sa.at(turn, s))
                    marked(f"sp_exp{c}", sa.step(a.activation(sp_exp[:, c], sp_exp[:, c], ACT.Exp, scale=-1.0).then_inc(sa.sem, 1)))
                for c in range(NCT):
                    act.wait_ge(sa.sem, sa.at(turn, mark[f"sp_exp{c}"]))
                    marked(f"sp_log{c}", sa.step(a.activation(sp_log[:, c], sp_exp[:, c], ACT.Ln, bias=1.0).then_inc(sa.sem, 1)))
                yield
                act.wait_ge(sp_.sem, sp_.named(turn, "decay_zero"))
                for unit in range(NU):
                    pair, c, slot = unit // NCT, unit % NCT, unit % 2
                    if unit >= 2:
                        act.wait_ge(decay_used.sem, decay_used.at(turn, unit - 1))
                    for n in range(2):
                        i = a.activation(decay[:, slot, n, 1:], dt[:, c, 1:], ACT.Exp,
                                         scale=a_neg[:, c, 2 * pair + n:2 * pair + n + 1])
                    i.then_inc(decay_ready.sem, 1)
                    yield

            def rest_part(turn):
                for c in range(NF):
                    act.wait_ge(B.ready.sem, B.filled_at(turn, ("zT", c)))
                    b = B.bank(("zT", c))
                    a.activation(xT[:, c], b[:, :], ACT.Identity, scale=ln1[:, c:c + 1])
                    a.activation(hT[:, c], b[:, :], ACT.Identity, scale=ln2[:, c:c + 1]).then_inc(B.freed_sem(("zT", c)), 1)
                for i in range(NQT):
                    empty(B, turn, ("q", i), qT[:, i], scale=HD ** -0.5)
                yield
                n = NT * HEADS
                for i in range(n + 2):
                    if i < n:
                        width = (i // HEADS + 1) * P
                        if i >= NPS:
                            act.wait_ge(B.ready.sem, B.filled_at(turn, ("PT", i - NPS)))
                        act.wait_ge(max_ready.sem, max_ready.at(turn, i + 1))
                        b = B.bank(("S", i))
                        a.activation(prob[:, i % NPS, 0:width], b[:, 0:width], ACT.Exp, bias=neg_max[:, i:i + 1], accum_out=prob_sum[:, i:i + 1]).then_inc(B.freed_sem(("S", i)), 1)
                    if i >= 2 and i % 2 == 0:
                        j = i - 2
                        width = (j // HEADS + 1) * P
                        if j >= NPS:
                            act.wait_ge(pv_done.sem, pv_done.at(turn, j - NPS + 1))
                        empty(B, turn, ("PT", j), probT[:, j % NPS, 0:width], src=lambda b: b[:, 0:width])
                    yield
                for c in range(NF):
                    empty(B, turn, ("oT", c), oT[:, c])
                empty(B, turn, ("mod", 0), tanhT, ACT.Tanh, src=lambda b: b[0:RANK, :])
                yield
                for f in range(NFT):
                    act.wait_ge(inner_ready.sem, inner_ready.at(turn, f - 1))
                    act.wait_ge(B.ready.sem, B.filled_at(turn, ("gate", f)))
                    b = B.bank(("gate", f))
                    i = a.activation(act_gate[:, f % 2], b[:, :], ACT.Silu)
                    i.then_inc(B.freed_sem(("gate", f)), 1)
                    yield
                for c in range(NF):
                    empty(B, turn, ("nT", c), xT[:, c])
                act.wait_ge(rv.sem, rv.named(turn, "mv1"))
                empty(B, turn, ("low", 0), lowT[0:RANK, :], src=lambda b: b[0:RANK, :])
                act.wait_ge(B.ready.sem, B.filled_at(turn, ("gk", 0)))
                b = B.bank(("gk", 0))
                s = ra.step(a.activation(g_abs, b[:, :], ACT.Abs, bias=g_bias).then_inc(ra.sem, 1))
                a.activation(g_relu, b[:, :], ACT.Relu, bias=g_nbias[:, :], scale=-1.0).then_inc(B.freed_sem(("gk", 0)), 1)
                act.wait_ge(ra.sem, ra.at(turn, s))
                s = marked("g_exp", ra.step(a.activation(g_abs, g_abs, ACT.Exp, scale=-1.0).then_inc(ra.sem, 1)))
                empty(B, turn, ("gq", 0), gq)
                empty(B, turn, ("gkey", 0), gkey)
                act.wait_ge(ra.sem, ra.at(turn, s))
                marked("g_log", ra.step(a.activation(g_log, g_abs, ACT.Ln, bias=1.0).then_inc(ra.sem, 1)))
                for i in range(2):
                    empty(B, turn, ("gg", i), gg[:, 2 * i:2 * i + 2], ACT.Silu,
                          src=lambda b: b[:, :].rearrange("p (t n) -> p t n", t=2))
                yield
                act.wait_ge(rv.sem, rv.named(turn, "cs"))
                ra.step(a.activation(e_q, cs, ACT.Exp, scale=-1.0 / 16).then_inc(ra.sem, 1))
                marked("e_kg", ra.step(a.activation(e_kg, cs, ACT.Exp, scale=1.0 / 16).then_inc(ra.sem, 1)))
                act.wait_ge(rv.sem, rv.named(turn, "cs_rel"))
                ra.step(a.activation(e_kd, e_kd, ACT.Exp, scale=1.0 / 16).then_inc(ra.sem, 1))
                marked("g_dec", ra.step(a.activation(g_last[:, :], cs[:, CHUNK - 1:SEQ:CHUNK], ACT.Exp, scale=-1.0 / 16).then_inc(ra.sem, 1)))
                yield
                empty(B, turn, ("kdT", 0), kd_tok, src=lambda b: b[:, :].rearrange("p (t n) -> p t n", t=NT))
                yield
                for t in range(NT):
                    act.wait_ge(B.ready.sem, B.filled_at(turn, ("GO", t)))
                    b = B.bank(("GO", t))
                    s = ra.step(a.activation(go_sq[:, t], b[:, 0:GHV], ACT.Square).then_inc(ra.sem, 1))
                    a.activation(go[:, t], b[:, 0:GHV], ACT.Copy).then_inc(B.freed_sem(("GO", t)), 1)
                    marked(f"go_sq{t}", s)
                    yield
                for c in range(NF):
                    empty(B, turn, ("goT", c), goT[:, c])
                yield
                for c in range(NF):
                    empty(B, turn, ("mT", c), xT[:, c])
                yield
                act.wait_ge(rv.sem, rv.named(turn, "rt_lm"))
                marked("rt_e", ra.step(a.activation(rt["e"], rt["lm"], ACT.Exp).then_inc(ra.sem, 1)))
                empty(B, turn, ("wT", 0), shareT, src=lambda b: b[0:EXPERTS, :])
                yield
                for f in range(NFT, NWT):
                    act.wait_ge(inner_ready.sem, inner_ready.at(turn, f - 1))
                    act.wait_ge(B.ready.sem, B.filled_at(turn, ("gate", f)))
                    b = B.bank(("gate", f))
                    i = a.activation(act_gate[:, f % 2], b[:, :], ACT.Silu)
                    i.then_inc(B.freed_sem(("gate", f)), 1)
                    yield

            with act.Fori(0, BATCH) as turn:
                for _ in scan_part(turn):
                    pass
                for _ in rest_part(turn):
                    pass

        @block.vector
        def _(dve):
            d = nc.vector
            for signal in (A.freed["dve"], B.freed["dve"], d_free, xa_free, pair_used, inner_ready):
                dve.sem_inc(signal.sem, signal.per)
            dve.wait_ge(prep, 3)
            dve.wait_ge(consts, 1)
            dve.wait_ge(prep, 4)
            d.tensor_copy(wo_a, bank[2][:, 0:NF * RANK].rearrange("p (c r) -> p c r", c=NF)).then_inc(prep, 1)

            def bc2(ap, n):
                return ap.unsqueeze(2).broadcast_to([P, ap.shape[1], n])

            def norm_stats(steps, turn, src, st, mv_, name):
                for t in range(NT):
                    s = steps.step(d.bn_stats(st[:, t], src[:, t]).then_inc(steps.sem, 1))
                dve.wait_ge(steps.sem, steps.at(turn, s))
                apart(dve)
                for t in range(NT):
                    s = steps.step(d.bn_aggr(mv_[:, t], st[:, t]).then_inc(steps.sem, 1))
                return marked(name, s)

            def normalise(steps, turn, dst, src, mv_, r, s):
                dve.wait_ge(steps.sem, steps.at(turn, s))
                for t in range(NT):
                    s = steps.step(d.tensor_scalar(dst[:, t], src[:, t], mv_[:, t, 0:1], r[:, t:t + 1], ALU.subtract, ALU.mult).then_inc(steps.sem, 1))
                return s

            def scan_part(turn):
                dve.wait_ge(x_in.sem, x_in.at(turn, 16))
                s = norm_stats(sv, turn, xa, a_stats, a_mv, "a_mv")
                dve.wait_ge(sp_.sem, sp_.named(turn, "a_rs"))
                marked("xn", normalise(sv, turn, xn, xa, a_mv, a_rs, s))
                z = sv.step(d.memset(hid[:, :, 0:KCONV - 1], 0.0).then_inc(sv.sem, 1))
                dve.wait_ge(sv.sem, sv.at(turn, z))
                yield
                for c in range(NCT):
                    dve.wait_ge(A.freed_sem(("hid", c)), A.freed_at(turn, ("hid", c)))
                    s = sv.step(d.tensor_scalar(dt[:, c], hid[:, c, 0:SEQ], conv_w[:, c, 0:1], None, ALU.mult).then_inc(sv.sem, 1))
                    for k in range(1, KCONV):
                        dve.wait_ge(sv.sem, sv.at(turn, s))
                        s = sv.step(d.scalar_tensor_tensor(dt[:, c], hid[:, c, k:k + SEQ], conv_w[:, c, k:k + 1], dt[:, c], ALU.mult, ALU.add).then_inc(sv.sem, 1))
                    marked(f"conv{c}", s)
                    yield
                dve.wait_ge(sa.sem, sa.named(turn, "ssm_sq"))
                sv.step(d.tensor_reduce(a_ss[:, 0:NT], ssm_sq[:, :, 0:DTRANK], AX.X, ALU.add).then_inc(sv.sem, 1))
                s = sv.step(d.tensor_reduce(a_ss[:, NT:3 * NT].rearrange("p (t g) -> p t g", t=NT), ssm_sq[:, :, DTRANK:].rearrange("p t (g n) -> p t g n", g=2), AX.X, ALU.add).then_inc(sv.sem, 1))
                marked("a_ss", s)
                dve.wait_ge(sp_.sem, sp_.named(turn, "a_rr"))
                dve.wait_ge(A.freed_sem(("ssm", 1)), A.freed_at(turn, ("ssm", 1)))
                s = sv.step(d.tensor_tensor(ssm[:, :, 0:DTRANK], ssm[:, :, 0:DTRANK], bc2(a_ss[:, 0:NT], DTRANK), ALU.mult).then_inc(sv.sem, 1))
                for g in range(2):
                    s = sv.step(d.tensor_tensor(ssm[:, :, DTRANK + g * NSTATE:DTRANK + (g + 1) * NSTATE], ssm[:, :, DTRANK + g * NSTATE:DTRANK + (g + 1) * NSTATE], bc2(a_ss[:, NT + g:3 * NT:2], NSTATE), ALU.mult).then_inc(sv.sem, 1))
                marked("ssm_n", s)
                yield
                for c in range(NCT):
                    dve.wait_ge(sp_.sem, sp_.named(turn, f"dt{c}"))
                    s = sv.step(d.tensor_tensor(dtu[:, c], dt[:, c], u[:, c], ALU.mult).then_inc(sv.sem, 1))
                dve.wait_ge(sv.sem, sv.at(turn, s))
                dve.wait_ge(sp_.sem, sp_.named(turn, "decay_zero"))
                yield
                for unit in range(NU):
                    pair, c, slot = unit // NCT, unit % NCT, unit % 2
                    if c == 0:
                        dve.wait_ge(bc_in[pair % 2].sem, bc_in[pair % 2].at(turn, 16 * (pair // 2 + 1)))
                    if unit >= 2:
                        dve.wait_ge(unit_added.sem, unit_added.at(turn, unit - 1))
                    s = sv.step(d.tensor_tensor(drive[:, slot], dtu[:, c].unsqueeze(1).broadcast_to([P, 2, SEQ]), bc[:, pair % 2, 0], ALU.mult).then_inc(sv.sem, 1))
                    dve.wait_ge(sv.sem, sv.at(turn, s))
                    dve.wait_ge(decay_ready.sem, decay_ready.at(turn, unit + 1))
                    flat = drive[:, slot].rearrange("p n t -> p (n t)")
                    d.tensor_tensor_scan(flat, decay[:, slot].rearrange("p n t -> p (n t)"), flat, 0.0,
                                         ALU.mult, ALU.add).then_inc(decay_used.sem, 1)
                    dve.wait_ge(decay_used.sem, decay_used.at(turn, unit + 1))
                    i = d.tensor_tensor(drive[:, slot], drive[:, slot], bc[:, pair % 2, 1], ALU.mult)
                    i.then_inc(unit_done.sem, 1)
                    if c == NCT - 1:
                        dve.wait_ge(unit_done.sem, unit_done.at(turn, unit + 1))
                        dve.sem_inc(pair_used.sem, 1)
                    yield
                for c in range(NCT):
                    dve.wait_ge(unit_added.sem, unit_added.at(turn, NU - NCT + c + 1))
                    s = sv.step(d.scalar_tensor_tensor(yacc[:, c], u[:, c], skip[:, c:c + 1], yacc[:, c], ALU.mult, ALU.add).then_inc(sv.sem, 1))
                    dve.wait_ge(sv.sem, sv.at(turn, s))
                    s = sv.step(d.tensor_tensor(yacc[:, c], yacc[:, c], sgate[:, c], ALU.mult).then_inc(sv.sem, 1))
                    marked(f"y{c}", s)
                yield
                for i in range(2):
                    dve.wait_ge(A.ready.sem, A.filled_at(turn, ("out", i)))
                    b = A.bank(("out", i))
                    t = slice(2 * i, 2 * i + 2)
                    ins = d.tensor_tensor(xa[:, t], xa[:, t], b[:, :].rearrange("p (t n) -> p t n", t=2), ALU.add)
                    ins.then_inc(A.freed_sem(("out", i)), 1)
                yield

            def add_down(turn, use):
                for i in range(2):
                    t = slice(2 * i, 2 * i + 2)
                    s = rv.step(d.tensor_tensor(xb[:, t], xb[:, t], D[i][:, :].rearrange("p (t n) -> p t n", t=2), ALU.add).then_inc(rv.sem, 1))
                dve.wait_ge(rv.sem, rv.at(turn, s))
                dve.sem_inc(d_free.sem, 1)
                return s

            def rest_part(turn):
                dve.wait_ge(A.freed_sem(("out", 1)), A.freed_at(turn, ("out", 1)))
                s = norm_stats(rv, turn, xa, stats, mv, "mv0")
                dve.wait_ge(rp.sem, rp.named(turn, "rs0"))
                s = normalise(rv, turn, nrm, xa, mv, rs, s)
                dve.wait_ge(rv.sem, rv.at(turn, s))
                dve.wait_ge(out_stored.sem, out_stored.at(turn, 0))
                s = rv.step(d.tensor_tensor(xb, xa, nrm, ALU.add).then_inc(rv.sem, 1))
                dve.wait_ge(rv.sem, rv.at(turn, s))
                dve.sem_inc(xa_free.sem, 1)
                dve.wait_ge(rp.sem, rp.named(turn, "rs2"))
                for t in range(NT):
                    s = rv.step(d.tensor_scalar(nrm[:, t], nrm[:, t], rs2[:, t:t + 1], None, ALU.mult).then_inc(rv.sem, 1))
                marked("zn", s)
                yield
                for i in range(NQT):
                    dve.wait_ge(B.ready.sem, B.filled_at(turn, ("k", i)))
                    b = B.bank(("k", i))
                    d.tensor_copy(kT[:, i], b[:, :]).then_inc(B.freed_sem(("k", i)), 1)
                for i in range(2):
                    dve.wait_ge(B.ready.sem, B.filled_at(turn, ("v", i)))
                    b = B.bank(("v", i))
                    d.tensor_copy(v[:, 2 * i:2 * i + 2], b[:, :].rearrange("p (t n) -> p t n", t=2)).then_inc(B.freed_sem(("v", i)), 1)
                yield
                n = NT * HEADS

                def query_tile(t):
                    h = slice(t * HEADS, (t + 1) * HEADS)
                    dve.wait_ge(pv_done.sem, pv_done.at(turn, (t + 1) * HEADS))
                    s = rv.step(d.reciprocal(prob_sum[:, h], prob_sum[:, h]).then_inc(rv.sem, 1))
                    dve.wait_ge(rv.sem, rv.at(turn, s))
                    s = rv.step(d.tensor_tensor(o_tok[:, t].rearrange("p (h n) -> p h n", h=HEADS), D[t % 2][:, 0:HID].rearrange("p (h n) -> p h n", h=HEADS), bc2(prob_sum[:, h], HD), ALU.mult).then_inc(rv.sem, 1))
                    dve.wait_ge(rv.sem, rv.at(turn, s))
                    dve.sem_inc(d_free.sem, 1)
                    return s

                for i in range(n + 2):
                    if i < n:
                        width = (i // HEADS + 1) * P
                        dve.wait_ge(B.ready.sem, B.filled_at(turn, ("S", i)))
                        b = B.bank(("S", i))
                        d.tensor_reduce(neg_max[:, i:i + 1], b[:, 0:width], AX.X, ALU.max, negate=True)\
                            .then_inc(max_ready.sem, 1)
                    if i >= 2 and i % 2 == 1:
                        j = i - 2
                        width = (j // HEADS + 1) * P
                        if j >= NPS:
                            dve.wait_ge(pv_done.sem, pv_done.at(turn, j - NPS + 1))
                        dve.wait_ge(B.ready.sem, B.filled_at(turn, ("PT", j)))
                        b = B.bank(("PT", j))
                        d.tensor_copy(probT[:, j % NPS, 0:width], b[:, 0:width]).then_inc(B.freed_sem(("PT", j)), 1)
                    if i >= HEADS + 4 and (i - 4) % HEADS == 0:
                        query_tile((i - 4) // HEADS - 1)
                    yield
                s = query_tile(NT - 1)
                marked("att_done", s)
                yield
                dve.wait_ge(B.ready.sem, B.filled_at(turn, ("hA", 0)))
                b = B.bank(("hA", 0))
                dve.wait_ge(B.freed_sem(("mod", 0)), B.freed_at(turn, ("mod", 0)))
                ins = d.scalar_tensor_tensor(gmod, tanhT, 0.1, b[0:RANK, :], ALU.mult, ALU.mult)
                ins.then_inc(B.freed_sem(("hA", 0)), 1)
                yield
                for f in range(NFT):
                    dve.wait_ge(B.ready.sem, B.filled_at(turn, ("up", f)))
                    b = B.bank(("up", f))
                    dve.wait_ge(B.freed_sem(("gate", f)), B.freed_at(turn, ("gate", f)))
                    dve.wait_ge(down_done.sem, down_done.at(turn, f - 1))
                    s = rv.step(d.tensor_tensor(inner[:, f % 2], act_gate[:, f % 2], b[:, :], ALU.mult).then_inc(rv.sem, 1))
                    dve.wait_ge(rv.sem, rv.at(turn, s))
                    dve.sem_inc(B.freed["dve"].sem, 1)
                    dve.sem_inc(inner_ready.sem, 1)
                    yield
                dve.wait_ge(down_done.sem, down_done.at(turn, NFT))
                s = add_down(turn, 0)
                s = norm_stats(rv, turn, xb, stats, mv, "mv1")
                dve.wait_ge(rp.sem, rp.named(turn, "rs1"))
                marked("gn", normalise(rv, turn, nrm, xb, mv, rs, s))
                yield
                dve.wait_ge(rp.sem, rp.named(turn, "g_soft"))
                s = rv.step(d.tensor_tensor_scan(cs, chunk_starts[:, :], g_log, 0.0, ALU.mult, ALU.add).then_inc(rv.sem, 1))
                marked("cs", s)
                dve.wait_ge(rv.sem, rv.at(turn, s))
                last = cs[:, CHUNK - 1:SEQ:CHUNK]
                s = rv.step(d.tensor_tensor(e_kd.rearrange("p (c i) -> p c i", c=NCHUNK), cs.rearrange("p (c i) -> p c i", c=NCHUNK), bc2(last, CHUNK), ALU.subtract).then_inc(rv.sem, 1))
                marked("cs_rel", s)
                for i in range(2):
                    dve.wait_ge(B.ready.sem, B.filled_at(turn, ("gv", i)))
                    b = B.bank(("gv", i))
                    d.tensor_copy(gv[:, 2 * i:2 * i + 2], b[:, :].rearrange("p (t n) -> p t n", t=2)).then_inc(B.freed_sem(("gv", i)), 1)
                dve.wait_ge(ra.sem, ra.named(turn, "e_kg"))
                dve.wait_ge(B.freed_sem(("gkey", 0)), B.freed_at(turn, ("gkey", 0)))
                s = rv.step(d.scalar_tensor_tensor(gq, gq, GK ** -0.5, e_q, ALU.mult, ALU.mult).then_inc(rv.sem, 1))
                marked("qg", s)
                s = rv.step(d.tensor_tensor(kg, gkey, e_kg, ALU.mult).then_inc(rv.sem, 1))
                dve.wait_ge(ra.sem, ra.named(turn, "g_dec"))
                s = rv.step(d.tensor_tensor(e_kd, gkey, e_kd, ALU.mult).then_inc(rv.sem, 1))
                marked("kd", s)
                dve.wait_ge(rv.sem, rv.at(turn, s))
                yield
                for c in range(NCHUNK - 1):
                    dve.wait_ge(B.ready.sem, B.filled_at(turn, ("dS", c)))
                    b = B.bank(("dS", c))
                    ins = d.tensor_tensor(state[:, c + 1], b[:, 0:GHV], blockdiag[:, :], ALU.mult)
                    ins.then_inc(B.freed_sem(("dS", c)), 1)
                    dve.wait_ge(B.freed_sem(("dS", c)), B.freed_at(turn, ("dS", c)))
                    if c:
                        s = rv.step(d.scalar_tensor_tensor(state[:, c + 1], state[:, c], g_last[:, c:c + 1], state[:, c + 1], ALU.mult, ALU.add).then_inc(rv.sem, 1))
                        dve.wait_ge(rv.sem, rv.at(turn, s))
                marked("states", s)
                for t in range(NT):
                    dve.wait_ge(B.ready.sem, B.filled_at(turn, ("AT", t)))
                    b = B.bank(("AT", t))
                    d.tensor_tensor(at_m[:, t], b[:, 0:GH * CHUNK], tri[:, :], ALU.mult).then_inc(B.freed_sem(("AT", t)), 1)
                yield
                for t in range(NT):
                    dve.wait_ge(ra.sem, ra.named(turn, f"go_sq{t}"))
                    s = rv.step(d.tensor_reduce(g_ss[:, t * GH:(t + 1) * GH], go_sq[:, t].rearrange("p (h n) -> p h n", h=GH), AX.X, ALU.add).then_inc(rv.sem, 1))
                marked("g_ss", s)
                dve.wait_ge(rp.sem, rp.named(turn, "g_rr"))
                for t in range(NT):
                    dve.wait_ge(B.freed_sem(("GO", t)), B.freed_at(turn, ("GO", t)))
                    s = rv.step(d.tensor_tensor(go[:, t].rearrange("p (h n) -> p h n", h=GH), go[:, t].rearrange("p (h n) -> p h n", h=GH), bc2(g_ss[:, t * GH:(t + 1) * GH], GV), ALU.mult).then_inc(rv.sem, 1))
                dve.wait_ge(rv.sem, rv.at(turn, s))
                s = rv.step(d.tensor_tensor(go, go, gg, ALU.mult).then_inc(rv.sem, 1))
                marked("go", s)
                yield
                for i in range(2):
                    dve.wait_ge(B.ready.sem, B.filled_at(turn, ("gout", i)))
                    b = B.bank(("gout", i))
                    t = slice(2 * i, 2 * i + 2)
                    d.tensor_tensor(xb[:, t], xb[:, t], b[:, :].rearrange("p (t n) -> p t n", t=2), ALU.add).then_inc(B.freed_sem(("gout", i)), 1)
                dve.wait_ge(B.freed_sem(("gout", 1)), B.freed_at(turn, ("gout", 1)))
                s = norm_stats(rv, turn, xb, stats, mv, "mv2")
                dve.wait_ge(rp.sem, rp.named(turn, "rsm"))
                marked("mn", normalise(rv, turn, nrm, xb, mv, rs, s))
                yield
                dve.wait_ge(B.ready.sem, B.filled_at(turn, ("rt", 0)))
                b = B.bank(("rt", 0))
                by = lambda ap: ap.rearrange("p (t e) -> p t e", t=NT)
                top, need, total, v4 = (small[:, i * NT:(i + 1) * NT] for i in (0, 1, 2, 3))
                top8 = small[:, 4 * NT:12 * NT].rearrange("p (t n) -> p t n", t=NT)
                s = rv.step(d.tensor_reduce(top, by(b[:, 0:NE]), AX.X, ALU.max).then_inc(rv.sem, 1))
                dve.wait_ge(rv.sem, rv.at(turn, s))
                ins = d.tensor_tensor(by(rt["lm"]), by(b[:, 0:NE]), bc2(top, EXPERTS), ALU.subtract)
                ins.then_inc(B.freed_sem(("rt", 0)), 1)
                dve.wait_ge(B.freed_sem(("rt", 0)), B.freed_at(turn, ("rt", 0)))
                marked("rt_lm", rv.step(d.tensor_copy(total, top).then_inc(rv.sem, 1)))
                dve.wait_ge(ra.sem, ra.named(turn, "rt_e"))
                apart(dve)
                for t in range(NT):
                    s = rv.step(d.max(top8[:, t], rt["e"][:, t * EXPERTS:(t + 1) * EXPERTS]).then_inc(rv.sem, 1))
                dve.wait_ge(rv.sem, rv.at(turn, s))
                fourth = top8[:, :, TOPK - 1:TOPK].broadcast_to([P, NT, EXPERTS])
                rv.step(d.tensor_tensor(by(rt["gt"]), by(rt["e"]), fourth, ALU.is_gt).then_inc(rv.sem, 1))
                s = rv.step(d.tensor_tensor(by(rt["eq"]), by(rt["e"]), fourth, ALU.is_equal).then_inc(rv.sem, 1))
                dve.wait_ge(rv.sem, rv.at(turn, s))
                rv.step(d.tensor_reduce(need, by(rt["gt"]), AX.X, ALU.add).then_inc(rv.sem, 1))
                s = rv.step(d.tensor_tensor_scan(rt["pre"], expert_starts[:, :], rt["eq"], 0.0, ALU.mult, ALU.add).then_inc(rv.sem, 1))
                dve.wait_ge(rv.sem, rv.at(turn, s))
                s = rv.step(d.tensor_tensor(by(rt["pre"]), by(rt["pre"]), bc2(need, EXPERTS), ALU.add).then_inc(rv.sem, 1))
                dve.wait_ge(rv.sem, rv.at(turn, s))
                s = rv.step(d.scalar_tensor_tensor(rt["sel"], rt["pre"], float(TOPK), rt["eq"], ALU.is_le, ALU.mult).then_inc(rv.sem, 1))
                dve.wait_ge(rv.sem, rv.at(turn, s))
                s = rv.step(d.tensor_tensor(rt["sel"], rt["sel"], rt["gt"], ALU.add).then_inc(rv.sem, 1))
                dve.wait_ge(rv.sem, rv.at(turn, s))
                s = rv.step(d.tensor_tensor(rt["sel"], rt["sel"], rt["e"], ALU.mult).then_inc(rv.sem, 1))
                dve.wait_ge(rv.sem, rv.at(turn, s))
                s = rv.step(d.tensor_reduce(total, by(rt["sel"]), AX.X, ALU.add).then_inc(rv.sem, 1))
                dve.wait_ge(rv.sem, rv.at(turn, s))
                s = rv.step(d.reciprocal(total, total).then_inc(rv.sem, 1))
                dve.wait_ge(rv.sem, rv.at(turn, s))
                s = rv.step(d.tensor_tensor(by(rt["sel"]), by(rt["sel"]), bc2(total, EXPERTS), ALU.mult).then_inc(rv.sem, 1))
                marked("share", s)
                dve.wait_ge(B.freed_sem(("wT", 0)), B.freed_at(turn, ("wT", 0)))
                s = rv.step(d.tensor_copy(share[0:EXPERTS], shareT).then_inc(rv.sem, 1))
                dve.wait_ge(rv.sem, rv.at(turn, s))
                s = rv.step(d.tensor_tensor(shareT, shareT, share[0:EXPERTS], ALU.subtract).then_inc(rv.sem, 1))
                dve.wait_ge(rv.sem, rv.at(turn, s))
                rv.step(d.tensor_copy(share[EXPERTS:2 * EXPERTS], shareT).then_inc(rv.sem, 1))
                s = rv.step(d.tensor_copy(share_mid, shareT).then_inc(rv.sem, 1))
                dve.wait_ge(rv.sem, rv.at(turn, s))
                s = rv.step(d.tensor_tensor(share[2 * EXPERTS:], shareT, share_mid, ALU.subtract).then_inc(rv.sem, 1))
                marked("share3", s)
                yield
                for f in range(NFT, NWT):
                    dve.wait_ge(B.ready.sem, B.filled_at(turn, ("up", f)))
                    b = B.bank(("up", f))
                    dve.wait_ge(B.freed_sem(("gate", f)), B.freed_at(turn, ("gate", f)))
                    ins = d.tensor_tensor(act_gate[:, f % 2], act_gate[:, f % 2], b[:, :], ALU.mult)
                    ins.then_inc(B.freed_sem(("up", f)), 1)
                    dve.wait_ge(B.freed_sem(("up", f)), B.freed_at(turn, ("up", f)))
                    dve.wait_ge(B.ready.sem, B.filled_at(turn, ("share", f)))
                    b = B.bank(("share", f))
                    dve.wait_ge(down_done.sem, down_done.at(turn, f - 1))
                    s = rv.step(d.tensor_tensor(inner[:, f % 2], act_gate[:, f % 2], b[:, :], ALU.mult).then_inc(rv.sem, 1))
                    dve.wait_ge(rv.sem, rv.at(turn, s))
                    dve.sem_inc(B.freed["dve"].sem, 1)
                    dve.sem_inc(inner_ready.sem, 1)
                    yield
                dve.wait_ge(down_done.sem, down_done.at(turn, NWT))
                marked("x_out", add_down(turn, 1))
                yield

            with dve.Fori(0, BATCH) as turn:
                for _ in scan_part(turn):
                    pass
                for _ in rest_part(turn):
                    pass

        @block.tensor
        def _(pe):
            t_ = nc.tensor
            pe.sem_inc(down_done.sem, down_done.per)
            pe.wait_ge(weights_in, 80)
            pe.wait_ge(prep, 3)
            wo_n = area(0, SEQ).rearrange("p (c n) -> p c n", c=NF)
            for c in range(NF):
                for j in range(NF):
                    m = t_.matmul(bank[2][:, c * RANK:(c + 1) * RANK], wo_n[:, j, c * P:(c + 1) * P], mod_a[:, j],
                                  start=(j == 0), stop=(j == NF - 1))
            m.then_inc(prep, 1)
            pe.wait_ge(consts, 1)
            pe.wait_ge(prep, 5)

            def filled(ring, m):
                m.then_inc(ring.ready.sem, 1)

            def transposes(ring, turn, key, blocks):
                pe.wait_ge(ring.last_sem(key), ring.last_at(turn, key))
                b = ring.bank(key)
                for cols, src in blocks:
                    m = t_.transpose(b[0:src.shape[1], cols], src, ident[0:src.shape[0], 0:src.shape[0]])
                filled(ring, m)

            def to_features(ring, turn, name, src):
                for c in range(NF):
                    transposes(ring, turn, (name, c), [(slice(t * P, (t + 1) * P), src[:, t, c * P:(c + 1) * P]) for t in range(NT)])

            def product(ring, turn, key, pairs, rows=P, cols=slice(0, 512)):
                pe.wait_ge(ring.last_sem(key), ring.last_at(turn, key))
                b = ring.bank(key)
                for i, (lhsT, rhs) in enumerate(pairs):
                    m = t_.matmul(b[0:rows, cols], lhsT, rhs, start=(i == 0), stop=(i == len(pairs) - 1))
                filled(ring, m)

            def token_product(ring, turn, name, src, weights, width, parts):
                for i in range(2):
                    pe.wait_ge(ring.last_sem((name, i)), ring.last_at(turn, (name, i)))
                    b = ring.bank((name, i))
                    for j in range(2):
                        t = 2 * i + j
                        for c in range(parts):
                            m = t_.matmul(b[:, j * 256:j * 256 + width], src[:, c, t * P:(t + 1) * P], weights[:, c],
                                          start=(c == 0), stop=(c == parts - 1))
                    filled(ring, m)

            def scan_part(turn):
                pe.wait_ge(sv.sem, sv.named(turn, "xn"))
                to_features(A, turn, "T", xn)
                pe.wait_ge(A.freed_sem(("T", 1)), A.freed_at(turn, ("T", 1)))
                for n in range(2 * NCT):
                    product(A, turn, (("hid", "gate")[n // NCT], n % NCT),
                            [(m_in[:, c, n * P:(n + 1) * P], xnT[:, c]) for c in range(NF)])
                    yield
                pe.wait_ge(sa.sem, sa.named(turn, "u"))
                token_product(A, turn, "ssm", u, m_x, NSSM, NCT)
                yield
                pe.wait_ge(sv.sem, sv.named(turn, "ssm_n"))
                transposes(A, turn, ("dtT", 0), [(slice(t * P, (t + 1) * P), ssm[:, t, 0:DTRANK]) for t in range(NT)])
                transposes(A, turn, ("bcT", 0), [(slice(t * P, (t + 1) * P), ssm[:, t, DTRANK:]) for t in range(NT)])
                pe.wait_ge(A.freed_sem(("dtT", 0)), A.freed_at(turn, ("dtT", 0)))
                for c in range(NCT):
                    product(A, turn, ("dtp", c), [(m_dt[:, c * P:(c + 1) * P], dtnT[:, :])])
                yield
                pe.wait_ge(sv.sem, sv.named(turn, f"y{NCT - 1}"))
                token_product(A, turn, "out", yacc, m_out, HID, NCT)
                yield

            def down(turn, f, use, first, last):
                if first:
                    pe.wait_ge(d_free.sem, d_free.at(turn, use))
                pe.wait_ge(inner_ready.sem, inner_ready.at(turn, f + 1))
                slot = wslot[:, f % NSLOT]
                for t in range(NT):
                    m = t_.matmul(D[t // 2][:, (t % 2) * HID:(t % 2 + 1) * HID], inner[:, f % 2, t * P:(t + 1) * P],
                                  slot[:, 2 * NF * P:], start=(first and t % 2 == 0), stop=last, skip_group_check=True)
                m.then_inc(down_done.sem, 1)

            def mlp_tile(turn, f, src, extra):
                pe.wait_ge(w_in[f % NSLOT].sem, w_in[f % NSLOT].at(turn, 16 * (f // NSLOT + 1)))
                slot = wslot[:, f % NSLOT]
                for n, name in enumerate(("gate", "up")):
                    pairs = [(slot[:, (n * NF + c) * P:(n * NF + c + 1) * P], src[:, c]) for c in range(NF)]
                    product(B, turn, (name, f), pairs + (extra if n == 0 else []))

            def rest_part(turn):
                pe.wait_ge(rv.sem, rv.named(turn, "zn"))
                to_features(B, turn, "zT", nrm)
                pe.wait_ge(B.freed_sem(("zT", 1)), B.freed_at(turn, ("zT", 1)))
                for i in range(NQT):
                    product(B, turn, ("q", i), [(wq[:, c, i * P:(i + 1) * P], xT[:, c]) for c in range(NF)])
                for i in range(NQT):
                    product(B, turn, ("k", i), [(wk[:, c, i * P:(i + 1) * P], xT[:, c]) for c in range(NF)])
                token_product(B, turn, "v", xT, wv, HID, NF)
                yield
                pe.wait_ge(B.freed_sem(("q", NQT - 1)), B.freed_at(turn, ("q", NQT - 1)))
                pe.wait_ge(B.freed_sem(("v", 1)), B.freed_at(turn, ("v", 1)))
                n = NT * HEADS
                for i in range(n + 3):
                    if i < n:
                        t, h = i // HEADS, i % HEADS
                        rows, width = slice(32 * (h % HPT), 32 * (h % HPT) + HD), (t + 1) * P
                        pe.wait_ge(B.last_sem(("S", i)), B.last_at(turn, ("S", i)))
                        b = B.bank(("S", i))
                        t_.matmul(b[:, 0:width], qT[rows, h // HPT, t * P:width], kT[rows, h // HPT, 0:width], start=True, stop=False)
                        filled(B, t_.matmul(b[:, t * P:width], ident_b[:, :], causal[:, :], start=False, stop=True))
                    if 2 <= i < n + 2:
                        j = i - 2
                        pe.wait_ge(B.freed_sem(("S", j)), B.freed_at(turn, ("S", j)))
                        transposes(B, turn, ("PT", j), [(slice(k * P, (k + 1) * P), prob[:, j % NPS, k * P:(k + 1) * P])
                                                       for k in range(j // HEADS + 1)])
                    if i >= 3:
                        j = i - 3
                        t, h = j // HEADS, j % HEADS
                        if h == 0:
                            pe.wait_ge(d_free.sem, d_free.at(turn, max(0, t - 1)))
                        pe.wait_ge(B.freed_sem(("PT", j)), B.freed_at(turn, ("PT", j)))
                        for k in range(t + 1):
                            m = t_.matmul(D[t % 2][:, h * HD:(h + 1) * HD], probT[:, j % NPS, k * P:(k + 1) * P],
                                          v[:, k, h * HD:(h + 1) * HD], start=(k == 0), stop=(k == t))
                        m.then_inc(pv_done.sem, 1)
                    yield
                pe.wait_ge(rv.sem, rv.named(turn, "att_done"))
                to_features(B, turn, "oT", o_tok)
                pe.wait_ge(B.freed_sem(("oT", 1)), B.freed_at(turn, ("oT", 1)))
                product(B, turn, ("mod", 0), [(wo_a[:, c], oT[:, c]) for c in range(NF)], rows=RANK)
                product(B, turn, ("hA", 0), [(mod_a[:, c], hT[:, c]) for c in range(NF)], rows=RANK)
                yield
                pe.wait_ge(B.freed_sem(("hA", 0)), B.freed_at(turn, ("hA", 0)))
                for f in range(NFT + 1):
                    if f < NFT:
                        mlp_tile(turn, f, hT, [(modb[:, f * P:(f + 1) * P], gmod)])
                    if f:
                        down(turn, f - 1, NT, f == 1, f == NFT)
                    yield
                pe.wait_ge(rv.sem, rv.named(turn, "gn"))
                to_features(B, turn, "nT", nrm)
                pe.wait_ge(B.freed_sem(("nT", 1)), B.freed_at(turn, ("nT", 1)))
                product(B, turn, ("low", 0), [(g_gk1[:, c], xT[:, c]) for c in range(NF)], rows=RANK)
                pe.wait_ge(B.freed_sem(("low", 0)), B.freed_at(turn, ("low", 0)))
                product(B, turn, ("gk", 0), [(gk2[:, :], lowT[0:RANK, :])])
                product(B, turn, ("gq", 0), [(g_q[:, c], xT[:, c]) for c in range(NF)])
                product(B, turn, ("gkey", 0), [(g_k[:, c], xT[:, c]) for c in range(NF)])
                token_product(B, turn, "gv", xT, g_v, GHV, NF)
                token_product(B, turn, "gg", xT, g_g, GHV, NF)
                yield
                pe.wait_ge(rv.sem, rv.named(turn, "kd"))
                transposes(B, turn, ("kdT", 0), [(slice(t * P, (t + 1) * P), e_kd[:, t * P:(t + 1) * P]) for t in range(NT)])
                pe.wait_ge(B.freed_sem(("kdT", 0)), B.freed_at(turn, ("kdT", 0)))
                for c in range(NCHUNK - 1):
                    half = slice((c % 2) * CHUNK, (c % 2 + 1) * CHUNK)
                    product(B, turn, ("dS", c), [(kd_tok[half, c // 2], gv[half, c // 2])], cols=slice(0, GHV))
                pe.wait_ge(rp.sem, rp.named(turn, "qbd"))
                for t in range(NT):
                    pe.wait_ge(B.last_sem(("AT", t)), B.last_at(turn, ("AT", t)))
                    b = B.bank(("AT", t))
                    for j in range(2):
                        c = 2 * t + j
                        m = t_.matmul(b[j * CHUNK:(j + 1) * CHUNK, 0:GH * CHUNK], kg[:, c * CHUNK:(c + 1) * CHUNK],
                                      qbd[:, c].rearrange("p h i -> p (h i)"), start=True, stop=True)
                    filled(B, m)
                yield
                pe.wait_ge(rv.sem, rv.named(turn, "states"))
                for t in range(NT):
                    pe.wait_ge(B.freed_sem(("AT", t)), B.freed_at(turn, ("AT", t)))
                    pe.wait_ge(B.last_sem(("GO", t)), B.last_at(turn, ("GO", t)))
                    b = B.bank(("GO", t))
                    apart(pe)
                    for j in range(2):
                        c, half = 2 * t + j, slice(j * CHUNK, (j + 1) * CHUNK)
                        if c:
                            t_.matmul(b[half, 0:GHV], gq[:, c * CHUNK:(c + 1) * CHUNK], state[:, c], start=True, stop=False)
                        for h in range(GH):
                            m = t_.matmul(b[half, h * GV:(h + 1) * GV], at_m[half, t, h * CHUNK:(h + 1) * CHUNK],
                                          gv[half, t, h * GV:(h + 1) * GV], start=(c == 0), stop=(c == 0 or h == GH - 1))
                    filled(B, m)
                    yield
                pe.wait_ge(rv.sem, rv.named(turn, "go"))
                to_features(B, turn, "goT", go)
                pe.wait_ge(B.freed_sem(("goT", 1)), B.freed_at(turn, ("goT", 1)))
                token_product(B, turn, "gout", goT, g_o, HID, NF)
                yield
                pe.wait_ge(rv.sem, rv.named(turn, "mn"))
                to_features(B, turn, "mT", nrm)
                pe.wait_ge(B.freed_sem(("mT", 1)), B.freed_at(turn, ("mT", 1)))
                pe.wait_ge(B.last_sem(("rt", 0)), B.last_at(turn, ("rt", 0)))
                b = B.bank(("rt", 0))
                for t in range(NT):
                    for c in range(NF):
                        m = t_.matmul(b[:, t * EXPERTS:(t + 1) * EXPERTS], xT[:, c, t * P:(t + 1) * P], router[:, c],
                                      start=(c == 0), stop=(c == NF - 1))
                filled(B, m)
                yield
                pe.wait_ge(rv.sem, rv.named(turn, "share"))
                transposes(B, turn, ("wT", 0), [(slice(t * P, (t + 1) * P), rt["sel"][:, t * EXPERTS:(t + 1) * EXPERTS]) for t in range(NT)])
                pe.wait_ge(rv.sem, rv.named(turn, "share3"))
                for f in range(NFT, NWT + 1):
                    if f < NWT:
                        mlp_tile(turn, f, xT, [])
                        m = f - NFT
                        product(B, turn, ("share", f), [(select[:, m * P:(m + 1) * P], share)])
                    if f > NFT:
                        down(turn, f - 1, NT + 1, f == NFT + 1, f == NWT)
                    yield

            with pe.Fori(0, BATCH) as turn:
                for _ in scan_part(turn):
                    pass
                for _ in rest_part(turn):
                    pass

        for s in (sv, sp_, sa, rv, rp, ra):
            mark[s.name] = s.n
    return mark


def kernel(**inputs):
    import concourse.bacc as _bacc
    from concourse.bass_utils import run_bass_kernel_spmd as _run

    get = {k: np.ascontiguousarray(v) for k, v in inputs.items()}

    def rows(a):
        return a.reshape(a.shape[0] // P, P, -1).transpose(1, 0, 2).reshape(P, -1)

    def spaced(a):
        o = np.zeros((HID, HEADS, P // HPT), a.dtype)
        o[:, :, 0:HD] = a.T.reshape(HID, HEADS, HD)
        return rows(o.reshape(HID, -1))

    L0, F0, L1, M1 = "L0_attn_", "L0_ffn_", "L1_attn_", "L1_ffn_"
    packed = {
        "m_in": rows(get[L0 + "in_proj_w"]), "m_x": rows(get[L0 + "x_proj_w"]), "m_dt": get[L0 + "dt_proj_w"],
        "m_out": rows(get[L0 + "out_proj_w"]), "conv_w": rows(get[L0 + "conv_w"].reshape(INTER, KCONV)),
        "conv_b": rows(get[L0 + "conv_b"]), "dt_b": rows(get[L0 + "dt_proj_b"]), "a_log": rows(get[L0 + "A_log"]),
        "skip": rows(get[L0 + "D_param"]), "ln1": rows(get[F0 + "ln1_w"]), "ln2": rows(get[F0 + "ln2_w"]),
        "wq": spaced(get[F0 + "Wq"]), "wk": spaced(get[F0 + "Wk"]), "wv": rows(get[F0 + "Wv"].T), "mod_a": rows(get[F0 + "A"]),
        "g_q": rows(get[L1 + "Wq"]), "g_k": rows(get[L1 + "Wk"]), "g_v": rows(get[L1 + "Wv"]), "g_g": rows(get[L1 + "Wg"]),
        "g_gk1": rows(get[L1 + "Wgk1"]), "g_bias": get[L1 + "bgk2"].reshape(P, 1), "g_o": rows(get[L1 + "Wo"]),
        "router": rows(get[M1 + "router_w"].T),
    }
    w = np.concatenate([packed[n] for n, _ in RESIDENT], axis=1)

    def tiles(gate, up, down):
        n = gate.shape[0] // P
        part = lambda a: a.reshape(n, P, NF, P).transpose(0, 3, 2, 1).reshape(n, P, NF * P)
        return np.concatenate([part(gate), part(up), down.reshape(n, P, HID)], axis=2)

    wt = np.concatenate([
        tiles(get[F0 + "W_in_base"], get[F0 + "W_up_base"], get[F0 + "W_down"].T),
        tiles(get[M1 + "gate_w"].reshape(-1, HID), get[M1 + "up_w"].reshape(-1, HID),
              get[M1 + "down_w"].transpose(0, 2, 1).reshape(-1, HID)),
    ], axis=0)
    arrays = {"x": get[L0 + "x"], "w": w, "wt": wt, "mod_b": get[F0 + "B"], "wo": get[F0 + "Wo"],
              "g_gk2": get[L1 + "Wgk2"], "g_norm": get[L1 + "g_norm_weight"]}
    arrays = {k: np.ascontiguousarray(v) for k, v in arrays.items()}

    counted = {}
    for _ in range(2):
        nc = _bacc.Bacc("TRN2", target_bir_lowering=False, num_devices=1)
        args = {k: nc.dram_tensor(k, v.shape, mybir.dt.from_np(v.dtype), kind="ExternalInput").ap() for k, v in arrays.items()}
        args["out"] = nc.dram_tensor("out", (BATCH, SEQ, HID), F32, kind="ExternalOutput").ap()
        counted = build(nc, counted, **args)
    r = _run(nc, [arrays], core_ids=[0])
    return r.results[0]["out"]
```
